# Optimizing a Trainium2 kernel written in Bass

```python
import numpy as np
import jax
import jax.numpy as jnp

def _softmax(x, axis=-1):
    return jax.nn.softmax(x, axis=axis)

def _gelu(x):
    return jax.nn.gelu(x, approximate=True)

def _silu(x):
    return jax.nn.silu(x)

def _sigmoid(x):
    return jax.nn.sigmoid(x)

def _layernorm(x, axis=-1, eps=1e-05):
    m = jnp.mean(x, axis=axis, keepdims=True)
    v = jnp.var(x, axis=axis, keepdims=True)
    return (x - m) / jnp.sqrt(v + eps)

def _scatter_add(tgt, idx, src, axis=0):
    return tgt.at[idx].add(src)

def _segment_sum(src, seg, n):
    return jax.ops.segment_sum(src, seg, n)
kernel_name = 'mk_adaln_d1_jaxref_r4_6c4852'

def setup_inputs(seed: int=0):
    np.random.seed(seed)
    _w = jnp.asarray

    def _L0_attn_setup():
        import jax, jax.numpy as jnp
        import numpy as np
        D_MODEL = 256
        N_HEADS = 16
        HEAD_DIM = D_MODEL // N_HEADS
        BATCH = 4
        SEQ = 1024
        EPS = 1e-06

        def _feature_map(x):
            return jax.nn.elu(x) + 1.0
        key = jax.random.key(seed)
        ks = jax.random.split(key, 9)
        s = 1.0 / np.sqrt(D_MODEL)
        return {'x': jax.random.normal(ks[0], (BATCH, SEQ, D_MODEL), jnp.float32), 'Wq': jax.random.normal(ks[1], (D_MODEL, D_MODEL), jnp.float32) * s, 'bq': jnp.zeros((D_MODEL,), jnp.float32), 'Wk': jax.random.normal(ks[2], (D_MODEL, D_MODEL), jnp.float32) * s, 'bk': jnp.zeros((D_MODEL,), jnp.float32), 'Wv': jax.random.normal(ks[3], (D_MODEL, D_MODEL), jnp.float32) * s, 'bv': jnp.zeros((D_MODEL,), jnp.float32), 'Wo': jax.random.normal(ks[4], (D_MODEL, D_MODEL), jnp.float32) * s, 'bo': jnp.zeros((D_MODEL,), jnp.float32)}
    _L0_attn_in = _L0_attn_setup()

    def _L0_ffn_setup():
        import jax, jax.numpy as jnp
        import numpy as np
        B, S, D_MODEL, D_FF = (4, 512, 256, 1024)

        def _quantum_transform(hidden, theta, w_real, w_imag):
            imag = w_imag * jnp.sin(theta + hidden * 0.1)
            quantum_phase = jnp.cos(theta) * w_real + jnp.sin(theta) * w_imag
            return hidden + quantum_phase * imag * 0.1
        key = jax.random.key(seed)
        ks = jax.random.split(key, 8)
        return {'x': jax.random.normal(ks[0], (B, S, D_MODEL), dtype=jnp.float32), 'W1': jax.random.normal(ks[1], (D_MODEL, D_FF), dtype=jnp.float32) * (1.0 / np.sqrt(D_MODEL)), 'b1': jnp.zeros((D_FF,), dtype=jnp.float32), 'quantum_phases': jax.random.normal(ks[2], (D_FF,), dtype=jnp.float32) * (2.0 * np.pi), 'quantum_weights_real': jax.random.normal(ks[3], (D_FF,), dtype=jnp.float32) * 0.1, 'quantum_weights_imag': jax.random.normal(ks[4], (D_FF,), dtype=jnp.float32) * 0.1, 'W2': jax.random.normal(ks[5], (D_FF, D_MODEL), dtype=jnp.float32) * (1.0 / np.sqrt(D_FF)), 'b2': jnp.zeros((D_MODEL,), dtype=jnp.float32)}
    _L0_ffn_in = _L0_ffn_setup()
    _L0_c = _w((lambda *s: np.random.randn(*s).astype(np.float32) * 0.05)(8, 256))
    _L0_wmod = _w((lambda *s: np.random.randn(*s).astype(np.float32) * 0.05)(256, 6 * 256) * 256 ** (-0.5))
    _d = {'L0_attn_x': _L0_attn_in['x'], 'L0_attn_Wq': _L0_attn_in['Wq'], 'L0_attn_bq': _L0_attn_in['bq'], 'L0_attn_Wk': _L0_attn_in['Wk'], 'L0_attn_bk': _L0_attn_in['bk'], 'L0_attn_Wv': _L0_attn_in['Wv'], 'L0_attn_bv': _L0_attn_in['bv'], 'L0_attn_Wo': _L0_attn_in['Wo'], 'L0_attn_bo': _L0_attn_in['bo'], 'L0_ffn_W1': _L0_ffn_in['W1'], 'L0_ffn_b1': _L0_ffn_in['b1'], 'L0_ffn_quantum_phases': _L0_ffn_in['quantum_phases'], 'L0_ffn_quantum_weights_real': _L0_ffn_in['quantum_weights_real'], 'L0_ffn_quantum_weights_imag': _L0_ffn_in['quantum_weights_imag'], 'L0_ffn_W2': _L0_ffn_in['W2'], 'L0_ffn_b2': _L0_ffn_in['b2'], 'L0_c': _L0_c, 'L0_wmod': _L0_wmod}
    _x0 = _d['L0_attn_x']
    _d['L0_attn_x'] = jax.random.normal(jax.random.fold_in(jax.random.key(seed), 1), (8, 1024, 256), dtype=_x0.dtype)
    del _x0
    return _d

def reference(L0_attn_x, L0_attn_Wq, L0_attn_bq, L0_attn_Wk, L0_attn_bk, L0_attn_Wv, L0_attn_bv, L0_attn_Wo, L0_attn_bo, L0_ffn_W1, L0_ffn_b1, L0_ffn_quantum_phases, L0_ffn_quantum_weights_real, L0_ffn_quantum_weights_imag, L0_ffn_W2, L0_ffn_b2, L0_c, L0_wmod):

    def _L0_attn_ref(x, Wq, bq, Wk, bk, Wv, bv, Wo, bo):
        import jax, jax.numpy as jnp
        import numpy as np
        D_MODEL = 256
        N_HEADS = 16
        HEAD_DIM = D_MODEL // N_HEADS
        BATCH = 4
        SEQ = 1024
        EPS = 1e-06

        def _feature_map(x):
            return jax.nn.elu(x) + 1.0
        B, S, _ = x.shape
        q = (x @ Wq + bq).reshape(B, S, N_HEADS, HEAD_DIM).transpose(0, 2, 1, 3)
        k = (x @ Wk + bk).reshape(B, S, N_HEADS, HEAD_DIM).transpose(0, 2, 1, 3)
        v = (x @ Wv + bv).reshape(B, S, N_HEADS, HEAD_DIM).transpose(0, 2, 1, 3)
        q = _feature_map(q)
        k = _feature_map(k)
        kv = jnp.einsum('bhnd,bhne->bhde', k, v)
        out = jnp.einsum('bhnd,bhde->bhne', q, kv)
        k_sum = k.sum(axis=2)
        normalizer = jnp.einsum('bhnd,bhd->bhn', q, k_sum) + EPS
        out = out / normalizer[..., None]
        out = out.transpose(0, 2, 1, 3).reshape(B, S, D_MODEL)
        return out @ Wo + bo

    def _L0_ffn_ref(x, W1, b1, quantum_phases, quantum_weights_real, quantum_weights_imag, W2, b2):
        import jax, jax.numpy as jnp
        import numpy as np
        B, S, D_MODEL, D_FF = (4, 512, 256, 1024)

        def _quantum_transform(hidden, theta, w_real, w_imag):
            imag = w_imag * jnp.sin(theta + hidden * 0.1)
            quantum_phase = jnp.cos(theta) * w_real + jnp.sin(theta) * w_imag
            return hidden + quantum_phase * imag * 0.1
        hidden = jnp.einsum('bsd,df->bsf', x, W1) + b1
        q = _quantum_transform(hidden, quantum_phases, quantum_weights_real, quantum_weights_imag)
        act = jax.nn.relu(q)
        return jnp.einsum('bsf,fd->bsd', act, W2) + b2
    x = L0_attn_x
    mod = (_silu(L0_c) @ L0_wmod).reshape(L0_c.shape[0], 6, 1, -1)
    sa, ca, ga, sb, cb, gb = (mod[:, 0], mod[:, 1], mod[:, 2], mod[:, 3], mod[:, 4], mod[:, 5])
    ga = (2 * (ga >= 0) - 1) * jnp.maximum(jnp.abs(ga), 0.25)
    gb = (2 * (gb >= 0) - 1) * jnp.maximum(jnp.abs(gb), 0.25)
    h = _layernorm(x, axis=-1) * (1 + ca) + sa
    x = x + ga * _L0_attn_ref(h, L0_attn_Wq, L0_attn_bq, L0_attn_Wk, L0_attn_bk, L0_attn_Wv, L0_attn_bv, L0_attn_Wo, L0_attn_bo)
    h = _layernorm(x, axis=-1) * (1 + cb) + sb
    x = x + gb * _L0_ffn_ref(h, L0_ffn_W1, L0_ffn_b1, L0_ffn_quantum_phases, L0_ffn_quantum_weights_real, L0_ffn_quantum_weights_imag, L0_ffn_W2, L0_ffn_b2)
    return x

_drawn_inputs = setup_inputs


def setup_inputs(seed=0):
    import zlib

    import numpy as np

    out = dict(_drawn_inputs(seed))
    spreads = {'L0_attn_bq': (0.0, 2.0),
     'L0_attn_bk': (0.0, 2.0),
     'L0_attn_bv': (0.0, 0.315),
     'L0_attn_bo': (0.0, 0.331),
     'L0_ffn_b1': (0.0, 0.472),
     'L0_ffn_b2': (0.0, 0.335)}
    factors = {'L0_attn_Wq': 8.0,
     'L0_attn_Wk': 8.0,
     'L0_attn_Wv': 6.273,
     'L0_ffn_quantum_phases': 52.759,
     'L0_ffn_quantum_weights_real': 64.0,
     'L0_ffn_quantum_weights_imag': 43.873}
    for name, (base, spread) in spreads.items():
        noise = np.random.default_rng([zlib.crc32(name.encode()), seed]).standard_normal(out[name].shape)
        drawn = base * np.exp(spread * noise) if base else spread * noise
        out[name] = jnp.asarray(drawn.astype(out[name].dtype))
    for name, factor in factors.items():
        out[name] = (out[name] * factor).astype(out[name].dtype)
    return out
```

```python
import math
from contextlib import ExitStack

import concourse.bass as bass
from concourse import mybir

F32 = mybir.dt.float32
F32R = mybir.dt.float32r
I32 = mybir.dt.int32
ALU = mybir.AluOpType
ACT = mybir.ActivationFunctionType
AX = mybir.AxisListType

P = 128
BATCH, SEQ, D = 8, 1024, 256
HD = 16
F = 1024
ROWS = SEQ // P
TPG = 4
GPB = ROWS // TPG
N = TPG * P
GROUPS = BATCH * GPB
DC = D // P
FC = F // P
QK, QKV = 2 * D, 3 * D
NH = D // HD
LN_EPS, ATT_EPS = 1e-5, 1e-6
TURN = 2 * math.pi
SIN_SCALE = 6.28318500518798828125
TURN_HI = 6.28125
TURN_LO = TURN - TURN_HI
ROUND = 1.5 * 2 ** 23
CONSTS = 7
AHEAD = 4
XR = 4


def adaln_block(nc, x, Wq, bq, Wk, bk, Wv, bv, Wo, bo, W1, b1, theta, w_re, w_im, W2, b2, c, wmod, out):
    x_v = x.rearrange("b (p t) d -> b p t d", p=P)
    out_v = out.rearrange("b (p t) d -> b p t d", p=P)

    split_rows = nc.dram_tensor("split_rows", (BATCH, 2, QK + 2 * D), F32, kind="Internal").ap()
    full_rows = nc.dram_tensor("full_rows", (BATCH, 3, D), F32, kind="Internal").ap()

    ctx = ExitStack()
    with ctx:
        def sb(name, shape, dt=F32):
            return ctx.enter_context(nc.sbuf_tensor(name, shape, dt))

        def pb(name):
            return ctx.enter_context(nc.psum_tensor(name, [P, 512], F32))

        xr = sb("xr", [P, XR, ROWS, D])
        q_ring = sb("q_ring", [P, 2, ROWS, D])
        wqkv_hi, wqkv_lo = (sb(f"wqkv_{s}", [P, DC, QKV], F32R) for s in ("hi", "lo"))
        w1_hi, w1_lo = (sb(f"w1_{s}", [P, DC, F], F32R) for s in ("hi", "lo"))
        w2_hi, w2_lo = (sb(f"w2_{s}", [P, FC, D], F32R) for s in ("hi", "lo"))
        wo_sb = sb("wo_sb", [P, DC, D])
        stage = sb("stage", [P, 2048])
        ident = sb("ident", [P, P])
        ones = sb("ones", [P, P])
        mask = sb("mask", [P, P])
        ones2 = sb("ones2", [2, P], F32R)
        b2_rows = sb("b2_rows", [2, 2 * D], F32R)
        CW = 2 * FC + 2 * DC
        cst = sb("cst", [P, BATCH, CW])
        cur_f = sb("cur_f", [P, 2, 2 * FC])
        cur_a = sb("cur_a", [P, 2, DC])
        cur_b = sb("cur_b", [P, 2, DC])
        gcoef = sb("gcoef", [P, FC])
        expo = sb("expo", [P, TPG])
        qk_rows = sb("qk_rows", [2, QK], F32R)
        o_rows = sb("o_rows", [2, 2 * D], F32R)
        ga_b, gb_b, bv_b = sb("ga_b", [P, D]), sb("gb_b", [P, D]), sb("bv_b", [P, D])
        st_a = sb("st_a", [P, TPG, 6])
        mv_a = sb("mv_a", [P, TPG, 2])
        ve_a = sb("ve_a", [P, TPG])
        rs_a = sb("rs_a", [P, TPG])
        xn_a = sb("xn_a", [P, TPG, D])
        hT_hi, hT_lo = sb("hT_hi", [P, DC, N], F32R), sb("hT_lo", [P, DC, N], F32R)
        er = sb("er", [P, 2, QK])
        kf = sb("kf", [P, 2, D])
        k_hi, k_lo = sb("k_hi", [P, 2, D], F32R), sb("k_lo", [P, 2, D], F32R)
        VW = P + 2
        v_hi = sb("v_hi", [P, 2, DC, VW], F32R)
        v_lo = sb("v_lo", [P, 2, D], F32R)
        kvm = sb("kvm", [P, DC, P])
        kvx = sb("kvx", [P, DC, P])
        ksr = sb("ksr", [P, DC, P])
        kvT_ks = sb("kvT_ks", [P, 2 * D])
        mg = sb("mg", [P, 2 * D])
        m_hi, m_lo = sb("m_hi", [P, DC, D], F32R), sb("m_lo", [P, DC, D], F32R)
        qp = sb("qp", [P, TPG, D])
        nrm = sb("nrm", [P, TPG * NH])
        nre = sb("nre", [P, TPG * NH])
        rno = sb("rno", [P, TPG * NH])
        qT_hi, qT_lo = hT_hi, hT_lo
        st_b = sb("st_b", [P, TPG, 6])
        mv_b = sb("mv_b", [P, TPG, 2])
        ve_b = sb("ve_b", [P, TPG])
        rs_b = sb("rs_b", [P, TPG])
        xn_b = sb("xn_b", [P, TPG, D])
        h2_hi, h2_lo = sb("h2_hi", [P, 2, DC, N], F32R), sb("h2_lo", [P, 2, DC, N], F32R)
        yv = sb("yv", [P, N])
        rv = sb("rv", [P, N])
        kv_f = sb("kv_f", [P, N])
        fr = sb("fr", [P, N])
        sn = sb("sn", [P, N])
        tv = sb("tv", [P, N])
        tb = sb("tb", [P, N])
        a_hi, a_lo = sb("a_hi", [P, 2, N], F32R), sb("a_lo", [P, 2, N], F32R)
        zv = sb("zv", [P, TPG, D])
        cT = sb("cT", [P, DC, BATCH])
        ce = sb("ce", [P, DC, BATCH])
        cr = sb("cr", [P, DC, BATCH])
        csil = sb("csil", [P, DC, BATCH])
        modT = sb("modT", [P, 4, DC, BATCH])
        th = sb("th", [P, 12, FC])
        thi = sb("thi", [P, FC], I32)

        U = [pb("U0"), pb("U1")]
        Y = [pb("Y0"), pb("Y1")]
        KV, V = pb("KV"), pb("V")
        Q = [pb("Q0"), pb("Q1")]

        wm = q_ring[:, :, :, :].rearrange("p a t d -> p (a t d)")[:, 0:DC * 6 * D] \
            .rearrange("p (k n) -> p k n", k=DC)
        xn_rows = xn_b[0:BATCH, :, :].rearrange("p t d -> p (t d)")
        bias8, bo8 = xn_rows[:, 0:QKV], xn_rows[:, QKV:QKV + D]
        full8 = zv[0:BATCH, :, :].rearrange("p t d -> p (t d)")[:, 0:3 * D]
        sp_hi, sp_lo = a_hi[0:BATCH, :, :].rearrange("p a n -> p (a n)"), \
            a_lo[0:BATCH, :, :].rearrange("p a n -> p (a n)")
        g8, neg8, mag8, go8 = yv[0:BATCH, :], fr[0:BATCH, :], sn[0:BATCH, :], tv[0:BATCH, 0:2 * D]
        qk8 = tb[0:BATCH, :]
        b2f = kf[0:2, :, :].rearrange("p t d -> p (t d)")
        c8, th_rows = xn_a[0:BATCH, 0, :], xn_a[0:4 * FC, 1, 0:P]
        b2h = sb("b2h", [2, 2 * D], F32R)
        stage_qkv = stage[:, 0:DC * QKV].rearrange("p (k n) -> p k n", k=DC)
        stage_w1 = stage[:, :].rearrange("p (k n) -> p k n", k=DC)
        stage_w2 = stage[:, :].rearrange("p (k n) -> p k n", k=FC)

        def sem(name):
            return ctx.enter_context(nc.semaphore(name))

        ld_c, ld_wm, ld_qkv, ld_rows, ld_th, ld_wo, ld_w1, ld_w2, ld_b2 = (
            sem(n) for n in ("ld_c", "ld_wm", "ld_qkv", "ld_rows", "ld_th", "ld_wo", "ld_w1", "ld_w2", "ld_b2"))
        rows_out = sem("rows_out")
        consts, dve_link = sem("consts"), sem("dve_link")
        turned, ce_s, silu_s, mod_mm, modT_s, trig_s = (sem(n) for n in ("turned", "ce_s", "silu_s", "mod_mm", "modT_s", "trig_s"))
        bias_mm, b1_mm, rows_s, b2hi_s, spl_s = (sem(n) for n in ("bias_mm", "b1_mm", "rows_s", "b2hi_s", "spl_s"))
        fixed_s, cst_s, wqkv_hi_s, wqkv_lo_s, w1_hi_s, w1_lo_s, w2_hi_s, w2_lo_s = (
            sem(n) for n in ("fixed_s", "cst_s", "wqkv_hi_s", "wqkv_lo_s", "w1_hi_s", "w1_lo_s", "w2_hi_s", "w2_lo_s"))
        x_in, x_out0, x_out1 = sem("x_in"), sem("x_out0"), sem("x_out1")
        qk_rows_in, o_rows_in, prep_rows_in, gb_in = (
            sem(n) for n in ("qk_rows_in", "o_rows_in", "prep_rows_in", "gb_in"))
        cura_s, stat_a, aggr_a, ve_a_s, rs_a_s, xn_a_s = (
            sem(n) for n in ("cura_s", "stat_a", "aggr_a", "ve_a_s", "rs_a_s", "xn_a_s"))
        tr_a, hT_hi_s, hT_lo_s = sem("tr_a"), sem("hT_hi_s"), sem("hT_lo_s")
        qk_mm, v_mm, relu_s, exp_s, q_s, k_s = (sem(n) for n in ("qk_mm", "v_mm", "relu_s", "exp_s", "q_s", "k_s"))
        khi_s, klo_s, vhi_s, vlo_s, kv_mm = (sem(n) for n in ("khi_s", "klo_s", "vhi_s", "vlo_s", "kv_mm"))
        kv_rd, kv_ev, prep_tr, prep_cp, m_mm, mg_s, mhi_s, mlo_s = (
            sem(n) for n in ("kv_rd", "kv_ev", "prep_tr", "prep_cp", "m_mm", "mg_s", "mhi_s", "mlo_s"))
        q_mul, n_sum, n_eps, n_rec, q_sc = (sem(n) for n in ("q_mul", "n_sum", "n_eps", "n_rec", "q_sc"))
        tr_q, qT_hi_s, qT_lo_s, o_mm, x1_s = (sem(n) for n in ("tr_q", "qT_hi_s", "qT_lo_s", "o_mm", "x1_s"))
        curb_s, stat_b, aggr_b, ve_b_s, rs_b_s, xn_b_s = (
            sem(n) for n in ("curb_s", "stat_b", "aggr_b", "ve_b_s", "rs_b_s", "xn_b_s"))
        tr_h, h2_hi_s, h2_lo_s = sem("tr_h"), sem("h2_hi_s"), sem("h2_lo_s")
        curf_s, f1_mm, y_s, rv_s, kr_s, fr_s, sn_s, t_s, tb_s, ahi_s, alo_s, f2_mm = (
            sem(n) for n in ("curf_s", "f1_mm", "y_s", "rv_s", "kr_s", "fr_s", "sn_s", "t_s", "tb_s", "ahi_s", "alo_s", "f2_mm"))
        z_s, y_out = sem("z_s"), sem("y_out")

        block = ctx.enter_context(nc.Block())

        LEAD = AHEAD // GPB
        LAST_KV = GROUPS - AHEAD

        def windows(eng, window):
            for g in range(GPB):
                window(0, g, True, True, g > 0)
            with eng.Fori(1, BATCH - LEAD) as b:
                for g in range(GPB):
                    window(b, g, True, True, True)
            for b in range(BATCH - LEAD, BATCH):
                for g in range(GPB):
                    G = b * GPB + g
                    window(b, g, False, G + 1 < GROUPS, G <= LAST_KV)

        def stand_wait(eng, held, s, value):
            if not isinstance(value, int):
                eng.reg_mov(held, value)
                eng.wait_ge(consts, CONSTS)
                eng.wait_ge(s, held)
            else:
                eng.wait_ge(s, value)

        def is_first(b, g):
            return isinstance(b, int) and b == 0 and g == 0

        def is_last(b):
            return isinstance(b, int) and b == BATCH - 1

        @block.sync
        def _(sp):
            sp.dma_start(wm, wmod.rearrange("(k p) n -> p k n", p=P)).then_inc(ld_wm, 16)
            sp.dma_start(xr[:, 0, :, :], x_v[0]).then_inc(x_in, 16)
            for i, w in enumerate((Wq, Wk, Wv)):
                sp.dma_start(stage_qkv[:, :, i * D:(i + 1) * D],
                             w.rearrange("(k p) n -> p k n", p=P)).then_inc(ld_qkv, 16)
            sp.dma_start(wo_sb[:, :, :], Wo.rearrange("(k p) n -> p k n", p=P)).then_inc(ld_wo, 16)
            for b in range(1, XR):
                sp.wait_ge(x_in, 16 * b)
                sp.dma_start(xr[:, b, :, :], x_v[b]).then_inc(x_in, 16)
            sp.wait_ge(rows_s, 3)
            sp.dma_start(split_rows[:, 0, :], sp_hi.bitcast(F32)).then_inc(rows_out, 16)
            sp.dma_start(split_rows[:, 1, :], sp_lo.bitcast(F32)).then_inc(rows_out, 16)
            sp.dma_start(full_rows.rearrange("b r d -> b (r d)"), full8).then_inc(rows_out, 16)
            sp.wait_ge(rows_out, 48)

            def load_qk_rows(b):
                sp.dma_start(qk_rows[:, :].bitcast(F32), split_rows[b, :, 0:QK]).then_inc(qk_rows_in, 16)

            def load_o_rows(b):
                sp.dma_start(o_rows[:, :].bitcast(F32), split_rows[b, :, QK:QK + 2 * D]).then_inc(o_rows_in, 16)

            def load_prep_rows(b):
                sp.dma_start(ga_b[:, :], full_rows[b, 0:1, :].broadcast_to([P, D])).then_inc(prep_rows_in, 16)
                sp.dma_start(bv_b[:, :], full_rows[b, 2:3, :].broadcast_to([P, D])).then_inc(prep_rows_in, 16)

            def load_gb(b):
                sp.dma_start(gb_b[:, :], full_rows[b, 1:2, :].broadcast_to([P, D])).then_inc(gb_in, 16)

            load_qk_rows(0)
            load_prep_rows(0)
            load_o_rows(0)
            load_gb(0)
            sp.wait_ge(wqkv_hi_s, 1)
            sp.wait_ge(wqkv_lo_s, 1)
            sp.wait_ge(bias_mm, 2)
            sp.dma_start(stage_w1, W1.rearrange("(k p) n -> p k n", p=P)).then_inc(ld_w1, 16)
            sp.wait_ge(w1_hi_s, 1)
            sp.wait_ge(w1_lo_s, 1)
            sp.wait_ge(b1_mm, 1)
            sp.dma_start(stage_w2, W2.rearrange("(k p) n -> p k n", p=P)).then_inc(ld_w2, 16)
            sp.wait_ge(qk_mm, TPG * GPB)
            load_qk_rows(1)
            sp.wait_ge(mg_s, 1)
            load_prep_rows(1)
            sp.wait_ge(qk_mm, 2 * TPG * GPB)
            load_qk_rows(2)

            def batch(b, left):
                G = b * GPB
                if left >= 1:
                    sp.wait_ge(o_mm, 2 * G + 4)
                    load_o_rows(b + 1)
                if left >= 2:
                    sp.wait_ge(mg_s, b + 2)
                    load_prep_rows(b + 2)
                sp.wait_ge(y_out, TPG * (G + 1))
                sp.dma_start(out_v[b, :, 0:TPG, :], xr[:, b % XR, 0:TPG, :]).then_inc(x_out0, 16)
                if left >= 3:
                    sp.wait_ge(qk_mm, TPG * (G + AHEAD + GPB))
                    load_qk_rows(b + 3)
                if left >= 1:
                    sp.wait_ge(z_s, 2 * G + 4)
                    load_gb(b + 1)
                sp.wait_ge(y_out, TPG * (G + 2))
                sp.dma_start(out_v[b, :, TPG:ROWS, :], xr[:, b % XR, TPG:ROWS, :]).then_inc(x_out1, 16)
                if left >= XR:
                    sp.wait_ge(x_out0, 16 * (b + 1))
                    sp.wait_ge(x_out1, 16 * (b + 1))
                    sp.wait_ge(x_in, 16 * (b + XR))
                    sp.dma_start(xr[:, b % XR, :, :], x_v[b + XR]).then_inc(x_in, 16)

            with sp.Fori(0, BATCH - XR) as b:
                batch(b, XR)
            for b in range(BATCH - XR, BATCH):
                batch(b, BATCH - 1 - b)
            sp.wait_ge(x_out0, 16 * BATCH)
            sp.wait_ge(x_out1, 16 * BATCH)

        @block.gpsimd
        def _(gp):
            held = gp.alloc_register("held")
            gp.dma_start(b2f, b2.rearrange("(o a n) -> o a n", o=1, a=1).broadcast_to([2, 2, D])).then_inc(ld_b2, 16)
            for i, v in enumerate((bq, bk, bv, bo)):
                gp.dma_start(xn_rows[:, i * D:(i + 1) * D],
                             v.rearrange("(o n) -> o n", o=1).broadcast_to([BATCH, D])).then_inc(ld_rows, 16)
            for i, v in enumerate((theta, w_re, w_im, b1)):
                gp.dma_start(th_rows[i * FC:(i + 1) * FC, :], v.rearrange("(f p) -> f p", p=P)).then_inc(ld_th, 16)
            made = [0]

            def make(i):
                made[0] += 1
                i.then_inc(consts, 1)
                gp.wait_ge(consts, made[0])

            make(gp.memset(ident[:, :], 0.0))
            make(gp.affine_select(out=ident[:, :], in_=ident[:, :], compare_op=ALU.not_equal, fill=1.0,
                                  base=0, pattern=[[-1, P]], channel_multiplier=1))
            make(gp.memset(ones[:, :], 1.0))
            make(gp.memset(expo[:, :], -0.5))
            make(gp.memset(mask[:, :], 1.0))
            heads = mask[:, :].rearrange("p (j e) -> p j e", e=HD)
            make(gp.affine_select(out=heads, in_=heads, compare_op=ALU.is_ge, fill=0.0, base=0,
                                  pattern=[[-HD, P // HD], [0, HD]], channel_multiplier=1))
            make(gp.affine_select(out=heads, in_=heads, compare_op=ALU.is_ge, fill=0.0, base=HD - 1,
                                  pattern=[[HD, P // HD], [0, HD]], channel_multiplier=-1))
            assert made[0] == CONSTS

            def rstd_a(H):
                stand_wait(gp, held, aggr_a, TPG * H + TPG)
                gp.tensor_scalar(ve_a[:, :], mv_a[:, :, 1], 1.0, LN_EPS, ALU.mult, ALU.add).then_inc(ve_a_s, 1)
                gp.wait_ge(ve_a_s, H + 1)
                gp.tensor_tensor(rs_a[:, :], ve_a[:, :], expo[:, :], ALU.pow).then_inc(rs_a_s, 1)

            def rstd_b(J):
                stand_wait(gp, held, aggr_b, TPG * J + TPG)
                gp.tensor_scalar(ve_b[:, :], mv_b[:, :, 1], 1.0, LN_EPS, ALU.mult, ALU.add).then_inc(ve_b_s, 1)
                gp.wait_ge(ve_b_s, J + 1)
                gp.tensor_tensor(rs_b[:, :], ve_b[:, :], expo[:, :], ALU.pow).then_inc(rs_b_s, 1)

            def k_low(H, pair):
                gp.wait_ge(khi_s, 2 * H + pair + 1)
                first = isinstance(H, int) and H == 0 and pair == 0
                if not first:
                    gp.wait_ge(kv_mm, TPG * H + 2 * pair)
                gp.tensor_tensor(k_lo[:, :, :], kf[:, :, :], k_hi[:, :, :].bitcast(F32),
                                 ALU.subtract).then_inc(klo_s, 1)

            def q_times_ksum(J, b, g):
                gp.wait_ge(q_s, TPG * J + TPG)
                gp.wait_ge(prep_cp, b + 1)
                if not (isinstance(J, int) and J == 0):
                    stand_wait(gp, held, tr_q, 2 * J)
                for t in range(TPG):
                    gp.tensor_tensor(qp[:, t, :], q_ring[:, b % 2, g * TPG + t, :],
                                     kvT_ks[:, D:2 * D], ALU.mult).then_inc(q_mul, 1)

            def q_scale(J, b, g):
                stand_wait(gp, held, n_rec, J + 1)
                for t in range(TPG):
                    gp.tensor_tensor(qp[:, t, :].rearrange("p (h e) -> p h e", e=HD),
                                     q_ring[:, b % 2, g * TPG + t, :].rearrange("p (h e) -> p h e", e=HD),
                                     rno[:, t * NH:(t + 1) * NH].unsqueeze(2).broadcast_to([P, NH, HD]),
                                     ALU.mult).then_inc(q_sc, 1)

            def fraction(c):
                gp.wait_ge(kr_s, c + 1)
                gp.tensor_tensor(fr[:, :], yv[:, :], kv_f[:, :], ALU.subtract).then_inc(fr_s, 1)

            def add_bias(c, g, f):
                stand_wait(gp, held, t_s, c + 1)
                gp.tensor_scalar(tb[:, :], tv[:, :], 1.0, cur_f[:, g, FC + f:FC + f + 1],
                                 ALU.mult, ALU.add).then_inc(tb_s, 1)

            def residual(G, b, g):
                stand_wait(gp, held, z_s, 2 * G + 2)
                for t in range(TPG):
                    place = xr[:, b % XR, g * TPG + t, :]
                    gp.tensor_tensor(place, zv[:, t, :], place, ALU.add).then_inc(y_out, 1)

            for H in range(AHEAD):
                rstd_a(H)
                k_low(H, 0)
                k_low(H, 1)
            q_times_ksum(0, 0, 0)
            q_scale(0, 0, 0)
            rstd_b(0)

            def window(b, g, do_a, do_b, do_kv):
                G = b * GPB + g
                J, H, C = G + 1, G + AHEAD, G * FC
                bj, gj = (b, 1) if g == 0 else (b + 1, 0)
                first = is_first(b, g)
                for f in range(FC):
                    c = C + f
                    if f > 0:
                        add_bias(c - 1, g, f - 1)
                    elif not first:
                        add_bias(c - 1, 1 - g, FC - 1)
                    fraction(c)
                    if f == 0 and do_b:
                        q_times_ksum(J, bj, gj)
                    if f == 1 and do_kv:
                        k_low(H - 1, 1)
                    if f == 1 and do_b:
                        q_scale(J, bj, gj)
                    if f == 2 and do_a:
                        rstd_a(H)
                    if f == 2 and not first:
                        residual(G - 1, *((b, 0) if g else (b - 1, 1)))
                    if f == 5 and do_b:
                        rstd_b(J)
                    if f == 7 and do_a:
                        k_low(H, 0)

            windows(gp, window)
            add_bias(GROUPS * FC - 1, 1, FC - 1)
            residual(GROUPS - 1, BATCH - 1, 1)

        @block.scalar
        def _(act):
            act.dma_start(c8, c).then_inc(ld_c, 16)
            act.wait_ge(turned, 1)
            act.activation(ce[:, :, :].rearrange("p k b -> p (k b)"), Y[0][:, 0:DC * BATCH], ACT.Exp,
                           scale=-1.0).then_inc(ce_s, 1)
            act.wait_ge(trig_s, 2)
            act.activation(th[:, 8:10, :], th[:, 6:8, :], ACT.Sin, scale=SIN_SCALE).then_inc(trig_s, 1)
            act.wait_ge(ld_qkv, 48)
            act.activation(wqkv_hi[:, :, :], stage_qkv, ACT.Copy).then_inc(wqkv_hi_s, 1)
            act.wait_ge(ld_b2, 16)
            act.activation(b2h[:, :], b2f, ACT.Copy).then_inc(b2hi_s, 1)

            def hT_high(H, ch, g):
                act.wait_ge(tr_a, 2 * H + ch + 1)
                if ch == 0:
                    act.wait_ge(cura_s, H + 1)
                act.activation(hT_hi[:, ch, :], Q[ch][:, :], ACT.Identity,
                               scale=cur_a[:, g, ch:ch + 1]).then_inc(hT_hi_s, 1)

            def exps(H, pair):
                for t in (2 * pair, 2 * pair + 1):
                    act.wait_ge(qk_mm, TPG * H + t + 1)
                    if not (isinstance(H, int) and H == 0 and pair == 0):
                        act.wait_ge(k_s, TPG * H + t - 1)
                    act.activation(er[:, t % 2, :], Q[t % 2][:, :], ACT.Relu, scale=-1.0).then_inc(relu_s, 1)
                for t in (2 * pair, 2 * pair + 1):
                    act.wait_ge(relu_s, TPG * H + t + 1)
                    act.activation(er[:, t % 2, :], er[:, t % 2, :], ACT.Exp, scale=-1.0).then_inc(exp_s, 1)

            def kv_high(H, pair):
                first = isinstance(H, int) and H == 0 and pair == 0
                act.wait_ge(v_mm, 2 * H + pair + 1)
                if first:
                    act.wait_ge(fixed_s, 2)
                else:
                    act.wait_ge(kv_mm, TPG * H + 2 * pair)
                act.activation(v_hi[:, :, :, 0:P], V[:, :].rearrange("p (t h e) -> p t h e", t=2, h=DC),
                               ACT.Copy).then_inc(vhi_s, 1)
                act.wait_ge(k_s, TPG * H + 2 * pair + 2)
                act.activation(k_hi[:, :, :], kf[:, :, :], ACT.Copy).then_inc(khi_s, 1)

            def copy_prep(b, J):
                act.wait_ge(prep_tr, b + 1)
                if J is not None:
                    act.wait_ge(q_mul, TPG * J + TPG)
                act.activation(kvT_ks[:, :], V[:, :], ACT.Copy).then_inc(prep_cp, 1)

            def m_high(b):
                act.wait_ge(mg_s, b + 1)
                act.activation(m_hi[:, :, :], mg[:, :].rearrange("p (h n) -> p h n", h=DC),
                               ACT.Copy).then_inc(mhi_s, 1)

            def qT_high(J, ch):
                act.wait_ge(tr_q, 2 * J + ch + 1)
                act.activation(qT_hi[:, ch, :], Q[ch][:, :], ACT.Copy).then_inc(qT_hi_s, 1)

            def h2_high(J, ch, g):
                act.wait_ge(tr_h, 2 * J + ch + 1)
                act.wait_ge(curb_s, J + 1)
                act.activation(h2_hi[:, g, ch, :], Q[ch][:, :], ACT.Identity,
                               scale=cur_b[:, g, ch:ch + 1]).then_inc(h2_hi_s, 1)

            def whole_turns(c):
                act.wait_ge(y_s, c + 1)
                act.activation(rv[:, :], yv[:, :], ACT.Copy, bias=ROUND).then_inc(rv_s, 1)
                act.wait_ge(rv_s, c + 1)
                act.activation(kv_f[:, :], rv[:, :], ACT.Copy, bias=-ROUND).then_inc(kr_s, 1)

            def sine(c):
                act.wait_ge(fr_s, c + 1)
                act.activation(sn[:, :], fr[:, :], ACT.Sin, scale=SIN_SCALE).then_inc(sn_s, 1)

            def act_high(c, f, few):
                act.wait_ge(tb_s, c + 1)
                if not few:
                    act.wait_ge(f2_mm, c - 1)
                act.activation(a_hi[:, f % 2, :], tb[:, :], ACT.Relu).then_inc(ahi_s, 1)

            for H in range(AHEAD):
                hT_high(H, 0, H % 2)
                hT_high(H, 1, H % 2)
                exps(H, 0)
                kv_high(H, 0)
                if H == 0:
                    act.wait_ge(ld_w1, 16)
                    act.activation(w1_hi[:, :, :], stage_w1, ACT.Copy).then_inc(w1_hi_s, 1)
                if H == 1:
                    act.wait_ge(ld_w2, 16)
                    act.activation(w2_hi[:, :, :], stage_w2, ACT.Copy).then_inc(w2_hi_s, 1)
                exps(H, 1)
                kv_high(H, 1)
                if H == GPB - 1:
                    copy_prep(0, None)
                    m_high(0)
            qT_high(0, 0)
            qT_high(0, 1)
            h2_high(0, 0, 0)
            h2_high(0, 1, 0)

            def window(b, g, do_a, do_b, do_kv):
                G = b * GPB + g
                J, H, C = G + 1, G + AHEAD, G * FC
                first = is_first(b, g)
                for f in range(FC):
                    c = C + f
                    if not (first and f == 0):
                        act_high(c - 1, (f - 1) % FC, first and f <= 2)
                    if f == 0 and do_kv:
                        exps(H - 1, 1)
                    whole_turns(c)
                    if f == 2 and do_b:
                        qT_high(J, 0)
                        qT_high(J, 1)
                    if f == 4 and do_a:
                        hT_high(H, 0, g)
                        hT_high(H, 1, g)
                    sine(c)
                    if f == 1 and do_kv:
                        kv_high(H - 1, 1)
                    if f == 4 and g == 0 and not is_last(b):
                        copy_prep(b + 1, J)
                    if f == 5 and g == 0 and not is_last(b):
                        m_high(b + 1)
                    if f == 5 and do_a:
                        exps(H, 0)
                    if f == 6 and do_b:
                        h2_high(J, 0, 1 - g)
                        h2_high(J, 1, 1 - g)
                    if f == 6 and do_a:
                        kv_high(H, 0)

            windows(act, window)
            act_high(GROUPS * FC - 1, FC - 1, False)

        @block.vector
        def _(dve):
            held = dve.alloc_register("held")
            chain = [0]

            def link(i):
                chain[0] += 1
                i.then_inc(dve_link, 1)
                dve.wait_ge(dve_link, chain[0])

            dve.wait_ge(consts, CONSTS)
            dve.tensor_copy(ones2[:, :], ones[0:2, :]).then_inc(fixed_s, 1)
            dve.tensor_copy(v_hi[:, :, :, P:VW], ones[:, 0:8].rearrange("p (t h e) -> p t h e", t=2, h=DC)) \
                .then_inc(fixed_s, 1)
            dve.wait_ge(ce_s, 1)
            link(dve.tensor_copy(cT[:, :, :].rearrange("p k b -> p (k b)"), Y[0][:, 0:DC * BATCH]))
            link(dve.tensor_scalar(cr[:, :, :], ce[:, :, :], 1.0, None, ALU.add))
            link(dve.reciprocal(ce[:, :, :], cr[:, :, :]))
            dve.tensor_tensor(csil[:, :, :], cT[:, :, :], ce[:, :, :], ALU.mult).then_inc(silu_s, 1)
            dve.wait_ge(turned, 2)
            link(dve.tensor_copy(th[:, 0:4, :].rearrange("p v f -> p (v f)"), Y[1][:, 0:4 * FC]))
            link(dve.tensor_scalar(thi[:, :], th[:, 0, :], 1 / TURN, None, ALU.mult))
            link(dve.scalar_tensor_tensor(out=th[:, 4, :], in0=thi[:, :], scalar=-TURN_HI, in1=th[:, 0, :],
                                          op0=ALU.mult, op1=ALU.add))
            link(dve.scalar_tensor_tensor(out=th[:, 5, :], in0=thi[:, :], scalar=-TURN_LO, in1=th[:, 4, :],
                                          op0=ALU.mult, op1=ALU.add))
            link(dve.tensor_scalar(th[:, 10, :], th[:, 5, :], 1 / TURN, None, ALU.mult))
            link(dve.tensor_scalar(th[:, 11, :], th[:, 10, :], 0.25, None, ALU.add))
            for i in range(2):
                link(dve.tensor_copy(thi[:, :], th[:, 10 + i, :]))
                dve.tensor_tensor(th[:, 6 + i, :], th[:, 10 + i, :], thi[:, :], ALU.subtract).then_inc(trig_s, 1)
                dve.wait_ge(trig_s, i + 1)
            dve.wait_ge(trig_s, 3)
            link(dve.tensor_tensor(th[:, 10, :], th[:, 9, :], th[:, 1, :], ALU.mult))
            link(dve.tensor_tensor(th[:, 11, :], th[:, 8, :], th[:, 2, :], ALU.mult))
            link(dve.tensor_tensor(th[:, 0, :], th[:, 10, :], th[:, 11, :], ALU.add))
            link(dve.scalar_tensor_tensor(out=gcoef[:, :], in0=th[:, 0, :], scalar=0.1, in1=th[:, 2, :],
                                          op0=ALU.mult, op1=ALU.mult))
            dve.wait_ge(mod_mm, 2)
            dve.tensor_copy(modT[:, :, :, :].rearrange("p j k b -> p (j k b)"),
                            Q[1][:, 0:4 * DC * BATCH]).then_inc(modT_s, 1)
            link(dve.tensor_copy(g8, Q[0][0:BATCH, :]))
            link(dve.tensor_scalar(neg8, g8, -1.0, None, ALU.mult))
            link(dve.tensor_tensor(mag8, g8, neg8, ALU.max))
            link(dve.tensor_scalar(neg8, mag8, 0.25, None, ALU.max))
            link(dve.tensor_scalar(mag8, g8, 0.0, 2.0, ALU.is_ge, ALU.mult))
            link(dve.scalar_tensor_tensor(out=g8, in0=mag8, scalar=-1.0, in1=neg8, op0=ALU.add, op1=ALU.mult))
            link(dve.tensor_copy(full8[:, 0:2 * D], g8))
            dve.wait_ge(ld_rows, 64)
            for i in range(2):
                link(dve.tensor_tensor(go8[:, i * D:(i + 1) * D], g8[:, 0:D], bo8, ALU.mult))
            dve.wait_ge(bias_mm, 2)
            link(dve.tensor_tensor(qk8, Y[0][0:BATCH, :], bias8[:, 0:QK], ALU.add))
            dve.tensor_tensor(full8[:, 2 * D:3 * D], Y[1][0:BATCH, 0:D], bias8[:, QK:QKV], ALU.add) \
                .then_inc(rows_s, 1)
            link(dve.tensor_copy(sp_hi[:, 0:QK], qk8))
            link(dve.tensor_copy(sp_hi[:, QK:QK + 2 * D], go8))
            dve.tensor_tensor(sp_lo[:, 0:QK], qk8, sp_hi[:, 0:QK].bitcast(F32), ALU.subtract).then_inc(rows_s, 1)
            dve.tensor_tensor(sp_lo[:, QK:QK + 2 * D], go8, sp_hi[:, QK:QK + 2 * D].bitcast(F32),
                              ALU.subtract).then_inc(rows_s, 1)
            dve.wait_ge(wqkv_hi_s, 1)
            dve.tensor_tensor(wqkv_lo[:, :, :], stage_qkv, wqkv_hi[:, :, :].bitcast(F32), ALU.subtract) \
                .then_inc(wqkv_lo_s, 1)
            dve.wait_ge(modT_s, 1)
            for i, j in enumerate((1, 3)):
                link(dve.tensor_scalar(cst[:, :, 2 * FC + i * DC:2 * FC + (i + 1) * DC].rearrange("p b k -> p k b"),
                                       modT[:, j, :, :], 1.0, None, ALU.add))
            dve.wait_ge(b2hi_s, 1)
            link(dve.tensor_scalar(cr[0:2, 0, 0:1], ident[0:2, 1:2], -2.0, 1.0, ALU.mult, ALU.add))
            link(dve.tensor_scalar(zv[0:2, 3, :].unsqueeze(1).broadcast_to([2, 1, D])[:, 0, :],
                                   b2h[:, 0:D].bitcast(F32), cr[0:2, 0, 0:1], None, ALU.mult))
            for i in range(2):
                link(dve.scalar_tensor_tensor(out=b2_rows[:, i * D:(i + 1) * D], in0=b2f[:, i * D:(i + 1) * D],
                                              scalar=ident[0:2, 1:2], in1=zv[0:2, 3, :],
                                              op0=ALU.mult, op1=ALU.add))

            def stats_a(H, b, g):
                dve.tensor_copy(cur_a[:, g, :], cst[:, b, 2 * FC:2 * FC + DC]).then_inc(cura_s, 1)
                stand_wait(dve, held, x_in, 16 * b + 16)
                for t in range(TPG):
                    dve.bn_stats(st_a[:, t, :], xr[:, b % XR, g * TPG + t, :]).then_inc(stat_a, 1)
                stand_wait(dve, held, stat_a, TPG * H + TPG)
                for t in range(TPG):
                    dve.bn_aggr(mv_a[:, t, :], st_a[:, t, :]).then_inc(aggr_a, 1)

            def apply_a(H, b, g):
                dve.wait_ge(rs_a_s, H + 1)
                if not (isinstance(H, int) and H == 0):
                    dve.wait_ge(tr_a, 2 * H)
                for t in range(TPG):
                    dve.tensor_scalar(xn_a[:, t, :], xr[:, b % XR, g * TPG + t, :], mv_a[:, t, 0:1],
                                      rs_a[:, t:t + 1], ALU.subtract, ALU.mult).then_inc(xn_a_s, 1)

            def hT_low(H, ch, g):
                dve.wait_ge(hT_hi_s, 2 * H + ch + 1)
                dve.scalar_tensor_tensor(out=hT_lo[:, ch, :], in0=Q[ch][:, :], scalar=cur_a[:, g, ch:ch + 1],
                                         in1=hT_hi[:, ch, :].bitcast(F32), op0=ALU.mult,
                                         op1=ALU.subtract).then_inc(hT_lo_s, 1)

            def q_and_k(H, pair, b, g):
                for t in (2 * pair, 2 * pair + 1):
                    dve.wait_ge(exp_s, TPG * H + t + 1)
                    if t % 2 == 0 and not (isinstance(H, int) and H == 0 and pair == 0):
                        dve.wait_ge(klo_s, 2 * H + pair)
                    dve.scalar_tensor_tensor(out=q_ring[:, b % 2, g * TPG + t, :], in0=Q[t % 2][:, 0:D],
                                             scalar=0.0, in1=er[:, t % 2, 0:D], op0=ALU.max,
                                             op1=ALU.add).then_inc(q_s, 1)
                    dve.scalar_tensor_tensor(out=kf[:, t % 2, :], in0=Q[t % 2][:, D:QK],
                                             scalar=0.0, in1=er[:, t % 2, D:QK], op0=ALU.max,
                                             op1=ALU.add).then_inc(k_s, 1)

            def v_low(H, pair):
                dve.wait_ge(vhi_s, 2 * H + pair + 1)
                dve.tensor_tensor(v_lo[:, :, :].rearrange("p t (h e) -> p t h e", h=DC),
                                  V[:, :].rearrange("p (t h e) -> p t h e", t=2, h=DC),
                                  v_hi[:, :, :, 0:P].bitcast(F32), ALU.subtract).then_inc(vlo_s, 1)

            def read_kv(b):
                dve.wait_ge(kv_mm, ROWS * b + ROWS)
                dve.wait_ge(prep_rows_in, 32 * b + 32)
                for h in range(DC):
                    dve.scalar_tensor_tensor(out=kvx[:, h, :], in0=bv_b[:, h * P:(h + 1) * P],
                                             scalar=KV[:, h * 256 + P:h * 256 + P + 1],
                                             in1=KV[:, h * 256:h * 256 + P],
                                             op0=ALU.mult, op1=ALU.add).then_inc(kv_rd, 1)
                    dve.tensor_scalar(ksr[:, h, :], ones[:, :], KV[:, h * 256 + P:h * 256 + P + 1], None,
                                      ALU.mult).then_inc(kv_rd, 1)
                dve.wait_ge(kv_rd, 4 * b + 4)
                for h in range(DC):
                    dve.tensor_tensor(kvm[:, h, :], kvx[:, h, :], mask[:, :], ALU.mult).then_inc(kv_ev, 1)

            def gate_m(b):
                dve.wait_ge(m_mm, b + 1)
                dve.tensor_tensor(mg[:, :].rearrange("p (h n) -> p h n", h=DC),
                                  V[:, :].rearrange("p (h n) -> p h n", h=DC),
                                  ga_b[:, :].unsqueeze(1).broadcast_to([P, DC, D]), ALU.mult).then_inc(mg_s, 1)

            def m_low(b):
                dve.wait_ge(mhi_s, b + 1)
                dve.tensor_tensor(m_lo[:, :, :].rearrange("p h n -> p (h n)"), mg[:, :],
                                  m_hi[:, :, :].rearrange("p h n -> p (h n)").bitcast(F32),
                                  ALU.subtract).then_inc(mlo_s, 1)

            def normaliser(J):
                dve.wait_ge(q_mul, TPG * J + TPG)
                dve.tensor_reduce(out=nrm[:, :], in_=qp[:, :, :].rearrange("p t (h e) -> p (t h) e", e=HD),
                                  axis=AX.X, op=ALU.add).then_inc(n_sum, 1)
                dve.wait_ge(n_sum, J + 1)
                dve.tensor_scalar(nre[:, :], nrm[:, :], ATT_EPS, None, ALU.add).then_inc(n_eps, 1)
                dve.wait_ge(n_eps, J + 1)
                dve.reciprocal(rno[:, :], nre[:, :]).then_inc(n_rec, 1)

            def qT_low(J, ch):
                dve.wait_ge(qT_hi_s, 2 * J + ch + 1)
                dve.tensor_tensor(qT_lo[:, ch, :], Q[ch][:, :], qT_hi[:, ch, :].bitcast(F32),
                                  ALU.subtract).then_inc(qT_lo_s, 1)

            def add_x(J, pair, b, g):
                dve.wait_ge(o_mm, 2 * J + pair + 1)
                place = xr[:, b % XR, g * TPG + 2 * pair:g * TPG + 2 * pair + 2, :]
                dve.tensor_tensor(place, (V, Q[0])[pair][:, :].rearrange("p (t d) -> p t d", t=2), place,
                                  ALU.add).then_inc(x1_s, 1)

            def stats_b(J, b, g):
                dve.tensor_copy(cur_b[:, g, :], cst[:, b, 2 * FC + DC:CW]).then_inc(curb_s, 1)
                stand_wait(dve, held, x1_s, 2 * J + 2)
                for t in range(TPG):
                    dve.bn_stats(st_b[:, t, :], xr[:, b % XR, g * TPG + t, :]).then_inc(stat_b, 1)
                stand_wait(dve, held, stat_b, TPG * J + TPG)
                for t in range(TPG):
                    dve.bn_aggr(mv_b[:, t, :], st_b[:, t, :]).then_inc(aggr_b, 1)

            def apply_b(J, b, g):
                dve.wait_ge(rs_b_s, J + 1)
                if not (isinstance(J, int) and J == 0):
                    dve.wait_ge(tr_h, 2 * J)
                for t in range(TPG):
                    dve.tensor_scalar(xn_b[:, t, :], xr[:, b % XR, g * TPG + t, :], mv_b[:, t, 0:1],
                                      rs_b[:, t:t + 1], ALU.subtract, ALU.mult).then_inc(xn_b_s, 1)

            def h2_low(J, ch, g):
                dve.wait_ge(h2_hi_s, 2 * J + ch + 1)
                dve.scalar_tensor_tensor(out=h2_lo[:, g, ch, :], in0=Q[ch][:, :], scalar=cur_b[:, g, ch:ch + 1],
                                         in1=h2_hi[:, g, ch, :].bitcast(F32), op0=ALU.mult,
                                         op1=ALU.subtract).then_inc(h2_lo_s, 1)

            def turns(c, g, f):
                dve.wait_ge(f1_mm, c + 1)
                if not (isinstance(c, int) and c == 0):
                    dve.wait_ge(fr_s, c)
                dve.tensor_scalar(yv[:, :], U[f % 2][:, :], 0.1 / TURN, cur_f[:, g, f:f + 1],
                                  ALU.mult, ALU.add).then_inc(y_s, 1)

            def add_sine(c, f):
                dve.wait_ge(sn_s, c + 1)
                if not (isinstance(c, int) and c == 0):
                    dve.wait_ge(tb_s, c)
                dve.scalar_tensor_tensor(out=tv[:, :], in0=sn[:, :], scalar=gcoef[:, f:f + 1], in1=U[f % 2][:, :],
                                         op0=ALU.mult, op1=ALU.add).then_inc(t_s, 1)

            def act_low(c, f):
                dve.wait_ge(ahi_s, c + 1)
                dve.scalar_tensor_tensor(out=a_lo[:, f % 2, :], in0=tb[:, :], scalar=0.0,
                                         in1=a_hi[:, f % 2, :].bitcast(F32), op0=ALU.max,
                                         op1=ALU.subtract).then_inc(alo_s, 1)

            def gate_out(G, b):
                dve.wait_ge(f2_mm, FC * G + FC)
                dve.wait_ge(gb_in, 16 * b + 16)
                if not (isinstance(G, int) and G == 0):
                    dve.wait_ge(y_out, TPG * G)
                for p in range(2):
                    dve.tensor_tensor(zv[:, 2 * p:2 * p + 2, :], Y[p][:, :].rearrange("p (t d) -> p t d", t=2),
                                      gb_b[:, :].unsqueeze(1).broadcast_to([P, 2, D]),
                                      ALU.mult).then_inc(z_s, 1)

            for H in range(AHEAD):
                b, g = H // GPB, H % GPB
                stats_a(H, b, g)
                apply_a(H, b, g)
                hT_low(H, 0, g)
                hT_low(H, 1, g)
                q_and_k(H, 0, b, g)
                v_low(H, 0)
                if H == 0:
                    dve.wait_ge(w1_hi_s, 1)
                    dve.tensor_tensor(w1_lo[:, :, :], stage_w1, w1_hi[:, :, :].bitcast(F32), ALU.subtract) \
                        .then_inc(w1_lo_s, 1)
                if H == 1:
                    dve.wait_ge(b1_mm, 1)
                    link(dve.tensor_tensor(cst[:, :, FC:2 * FC].rearrange("p b f -> p f b"),
                                           U[0][:, 0:FC * BATCH].rearrange("p (f b) -> p f b", b=BATCH),
                                           th[:, 3, :].unsqueeze(2).broadcast_to([P, FC, BATCH]), ALU.add))
                    link(dve.scalar_tensor_tensor(out=cst[:, :, 0:FC], in0=cst[:, :, FC:2 * FC],
                                                  scalar=0.1 / TURN,
                                                  in1=th[:, 6, :].unsqueeze(1).broadcast_to([P, BATCH, FC]),
                                                  op0=ALU.mult, op1=ALU.add))
                    dve.wait_ge(w2_hi_s, 1)
                    dve.tensor_tensor(w2_lo[:, :, :], stage_w2, w2_hi[:, :, :].bitcast(F32), ALU.subtract) \
                        .then_inc(w2_lo_s, 1)
                q_and_k(H, 1, b, g)
                v_low(H, 1)
                if H == GPB - 1:
                    read_kv(0)
                    gate_m(0)
                    m_low(0)
            normaliser(0)
            qT_low(0, 0)
            qT_low(0, 1)
            add_x(0, 0, 0, 0)
            add_x(0, 1, 0, 0)
            stats_b(0, 0, 0)
            apply_b(0, 0, 0)
            h2_low(0, 0, 0)
            h2_low(0, 1, 0)

            def window(b, g, do_a, do_b, do_kv):
                G = b * GPB + g
                J, H, C = G + 1, G + AHEAD, G * FC
                bj, gj = (b, 1) if g == 0 else (b + 1, 0)
                bh = b + LEAD
                before = (b, 0) if g else (b - 1, 1)
                first = is_first(b, g)
                dve.tensor_copy(cur_f[:, g, :], cst[:, b, 0:2 * FC]).then_inc(curf_s, 1)
                dve.wait_ge(curf_s, G + 1)
                for f in range(FC):
                    c = C + f
                    turns(c, g, f)
                    if not (first and f == 0):
                        act_low(c - 1, (f - 1) % FC)
                    if f == 0 and do_kv:
                        q_and_k(H - 1, 1, b + LEAD - 1 if g == 0 else b + LEAD, 1 - g)
                    if f == 0 and do_a:
                        stats_a(H, bh, g)
                    if f == 1 and not first:
                        gate_out(G - 1, before[0])
                    if f == 2 and do_b:
                        qT_low(J, 0)
                        qT_low(J, 1)
                    if f == 4 and do_a:
                        hT_low(H, 0, g)
                        hT_low(H, 1, g)
                    add_sine(c, f)
                    if f == 1 and do_b:
                        normaliser(J)
                    if f == 1 and do_kv:
                        v_low(H - 1, 1)
                    if f == 3 and g == 0 and not is_last(b):
                        read_kv(b + 1)
                    if f == 3 and do_a:
                        apply_a(H, bh, g)
                    if f == 3 and do_b:
                        add_x(J, 0, bj, gj)
                        add_x(J, 1, bj, gj)
                    if f == 4 and do_b:
                        stats_b(J, bj, gj)
                    if f == 5 and g == 0 and not is_last(b):
                        gate_m(b + 1)
                        m_low(b + 1)
                    if f == 5 and do_b:
                        apply_b(J, bj, gj)
                    if f == 5 and do_a:
                        q_and_k(H, 0, bh, g)
                    if f == 6 and do_b:
                        h2_low(J, 0, 1 - g)
                        h2_low(J, 1, 1 - g)
                    if f == 6 and do_a:
                        v_low(H, 0)

            windows(dve, window)
            act_low(GROUPS * FC - 1, FC - 1)
            gate_out(GROUPS - 1, BATCH - 1)

        @block.tensor
        def _(pe):
            def passes(out, a, b, first, last):
                pe.matmul(out, a[0], b[0], start=first, stop=False)
                pe.matmul(out, a[0], b[1], start=False, stop=False)
                return pe.matmul(out, a[1], b[0], start=False, stop=last)

            pe.wait_ge(consts, 2)
            pe.wait_ge(ld_c, 16)
            for k in range(DC):
                last = pe.transpose(Y[0][:, k * BATCH:(k + 1) * BATCH], c8[:, k * P:(k + 1) * P],
                                    ident[0:BATCH, 0:BATCH])
            last.then_inc(turned, 1)
            pe.wait_ge(ld_th, 64)
            pe.transpose(Y[1][:, 0:4 * FC], th_rows, ident[0:4 * FC, 0:4 * FC]).then_inc(turned, 1)
            pe.wait_ge(silu_s, 1)
            pe.wait_ge(ld_wm, 16)
            for i, off in enumerate((2 * D, 5 * D)):
                for k in range(DC):
                    last = pe.matmul(Q[0][0:BATCH, i * D:(i + 1) * D], csil[:, k, :], wm[:, k, off:off + D],
                                     start=(k == 0), stop=(k == DC - 1))
            last.then_inc(mod_mm, 1)
            for j, off in enumerate((0, D, 3 * D, 4 * D)):
                for ch in range(DC):
                    at = (j * DC + ch) * BATCH
                    for k in range(DC):
                        last = pe.matmul(Q[1][:, at:at + BATCH], wm[:, k, off + ch * P:off + (ch + 1) * P],
                                         csil[:, k, :], start=(k == 0), stop=(k == DC - 1))
            last.then_inc(mod_mm, 1)
            pe.wait_ge(modT_s, 1)
            pe.wait_ge(ld_qkv, 48)
            for i, (o, off, n) in enumerate(((Y[0], 0, QK), (Y[1], QK, D))):
                for k in range(DC):
                    last = pe.matmul(o[0:BATCH, 0:n], modT[:, 0, k, :], stage_qkv[:, k, off:off + n],
                                     start=(k == 0), stop=(k == DC - 1))
                last.then_inc(bias_mm, 1)

            def transpose_a(H, window_group):
                pe.wait_ge(xn_a_s, TPG * H + TPG)
                if window_group is not None:
                    pe.wait_ge(x1_s, 2 * window_group + 4)
                elif not (isinstance(H, int) and H == 0):
                    pe.wait_ge(k_s, TPG * H)
                for ch in range(DC):
                    for t in range(TPG):
                        last = pe.transpose(Q[ch][:, t * P:(t + 1) * P], xn_a[:, t, ch * P:(ch + 1) * P], ident[:, :])
                    last.then_inc(tr_a, 1)

            def project(H, t, b):
                sl = slice(t * P, (t + 1) * P)
                for k in range(DC):
                    passes_hi = (k == 0)
                    if passes_hi:
                        pe.matmul(Q[t % 2][:, :], ones2[:, :], qk_rows[:, :], start=True, stop=False)
                    last = passes(Q[t % 2][:, :], (hT_hi[:, k, sl], hT_lo[:, k, sl]),
                                  (wqkv_hi[:, k, 0:QK], wqkv_lo[:, k, 0:QK]), False, k == DC - 1)
                last.then_inc(qk_mm, 1)
                for k in range(DC):
                    last = passes(V[:, (t % 2) * D:(t % 2 + 1) * D], (hT_hi[:, k, sl], hT_lo[:, k, sl]),
                                  (wqkv_hi[:, k, QK:QKV], wqkv_lo[:, k, QK:QKV]),
                                  t % 2 == 0 and k == 0, t % 2 == 1 and k == DC - 1)
                if t % 2:
                    last.then_inc(v_mm, 1)

            def sum_kv(H, pair, start, stop):
                pe.wait_ge(khi_s, 2 * H + pair + 1)
                pe.wait_ge(klo_s, 2 * H + pair + 1)
                pe.wait_ge(vlo_s, 2 * H + pair + 1)
                for t in range(2):
                    for h in range(DC):
                        hs = slice(h * P, (h + 1) * P)
                        o = KV[:, h * 256:h * 256 + VW]
                        pe.matmul(o, k_hi[:, t, hs], v_hi[:, t, h, :], start=start and t == 0 and h == 0, stop=False)
                        pe.matmul(o[:, 0:P], k_hi[:, t, hs], v_lo[:, t, hs], start=False, stop=False)
                        last = pe.matmul(o, k_lo[:, t, hs], v_hi[:, t, h, :], start=False,
                                         stop=stop and t == 1 and h == DC - 1)
                    last.then_inc(kv_mm, 1)

            def turn_kv(b):
                pe.wait_ge(kv_ev, 2 * b + 2)
                for h in range(DC):
                    pe.transpose(V[:, h * P:(h + 1) * P], kvm[:, h, :], ident[:, :])
                for h in range(DC):
                    last = pe.matmul(V[:, D + h * P:D + (h + 1) * P], ksr[:, h, :], ident[:, :],
                                     start=True, stop=True)
                last.then_inc(prep_tr, 1)

            def m_products(b):
                pe.wait_ge(prep_cp, b + 1)
                if isinstance(b, int) and b == 0:
                    pe.wait_ge(ld_wo, 16)
                for h in range(DC):
                    last = pe.matmul(V[:, h * D:(h + 1) * D], kvT_ks[:, h * P:(h + 1) * P], wo_sb[:, h, :],
                                     start=True, stop=True)
                last.then_inc(m_mm, 1)

            def transpose_q(J):
                pe.wait_ge(q_sc, TPG * J + TPG)
                for ch in range(DC):
                    for t in range(TPG):
                        last = pe.transpose(Q[ch][:, t * P:(t + 1) * P], qp[:, t, ch * P:(ch + 1) * P], ident[:, :])
                    last.then_inc(tr_q, 1)

            def attention_out(J, b):
                pe.wait_ge(qT_lo_s, 2 * J + 2)
                pe.wait_ge(mlo_s, b + 1)
                pe.wait_ge(o_rows_in, 16 * b + 16)
                for pair, o in enumerate((V, Q[0])):
                    pe.matmul(o[:, :], ones2[:, :], o_rows[:, :], start=True, stop=False)
                    for t in range(2):
                        sl = slice((2 * pair + t) * P, (2 * pair + t + 1) * P)
                        for k in range(DC):
                            last = passes(o[:, t * D:(t + 1) * D], (qT_hi[:, k, sl], qT_lo[:, k, sl]),
                                          (m_hi[:, k, :], m_lo[:, k, :]), False, t == 1 and k == DC - 1)
                    last.then_inc(o_mm, 1)

            def transpose_h(J):
                pe.wait_ge(xn_b_s, TPG * J + TPG)
                for ch in range(DC):
                    for t in range(TPG):
                        last = pe.transpose(Q[ch][:, t * P:(t + 1) * P], xn_b[:, t, ch * P:(ch + 1) * P], ident[:, :])
                    last.then_inc(tr_h, 1)

            def ffn_up(c, G, g, f):
                if f == 0:
                    pe.wait_ge(h2_lo_s, 2 * G + 2)
                if not (isinstance(c, int) and c < 2):
                    pe.wait_ge(t_s, c - 1)
                fs = slice(f * P, (f + 1) * P)
                for k in range(DC):
                    last = passes(U[f % 2][:, :], (w1_hi[:, k, fs], w1_lo[:, k, fs]),
                                  (h2_hi[:, g, k, :], h2_lo[:, g, k, :]), k == 0, k == DC - 1)
                last.then_inc(f1_mm, 1)

            def ffn_down(c, G, f):
                pe.wait_ge(alo_s, c + 1)
                if f == 0:
                    if not (isinstance(G, int) and G == 0):
                        pe.wait_ge(z_s, 2 * G)
                    for p in range(2):
                        pe.matmul(Y[p][:, :], ones2[:, :], b2_rows[:, :], start=True, stop=False)
                for t in range(TPG):
                    sl = slice(t * P, (t + 1) * P)
                    last = passes(Y[t // 2][:, (t % 2) * D:(t % 2 + 1) * D],
                                  (a_hi[:, f % 2, sl], a_lo[:, f % 2, sl]),
                                  (w2_hi[:, f, :], w2_lo[:, f, :]), False, f == FC - 1 and t % 2 == 1)
                last.then_inc(f2_mm, 1)

            pe.wait_ge(wqkv_lo_s, 1)
            for H in range(AHEAD):
                b, g = H // GPB, H % GPB
                transpose_a(H, None)
                pe.wait_ge(qk_rows_in, 16 * (b + 1))
                pe.wait_ge(hT_lo_s, 2 * H + 2)
                if H:
                    pe.wait_ge(vlo_s, 2 * H)
                project(H, 0, b)
                project(H, 1, b)
                if H == 0:
                    pe.wait_ge(ld_w1, 16)
                    for f in range(FC):
                        for k in range(DC):
                            last = pe.matmul(U[0][:, f * BATCH:(f + 1) * BATCH], stage_w1[:, k, f * P:(f + 1) * P],
                                             modT[:, 2, k, :], start=(k == 0), stop=(k == DC - 1))
                    last.then_inc(b1_mm, 1)
                pe.wait_ge(vlo_s, 2 * H + 1)
                pe.wait_ge(k_s, TPG * H + 1)
                project(H, 2, b)
                pe.wait_ge(k_s, TPG * H + 2)
                project(H, 3, b)
                sum_kv(H, 0, g == 0, False)
                sum_kv(H, 1, False, g == 1)
                if H == GPB - 1:
                    turn_kv(0)
                    m_products(0)
                    pe.wait_ge(mg_s, 1)
            pe.wait_ge(k_s, TPG * AHEAD)
            transpose_q(0)
            pe.wait_ge(vlo_s, 2 * AHEAD)
            attention_out(0, 0)
            transpose_h(0)

            def window(b, g, do_a, do_b, do_kv):
                G = b * GPB + g
                J, H, C = G + 1, G + AHEAD, G * FC
                bj = b if g == 0 else b + 1
                first = is_first(b, g)
                for f in range(FC):
                    c = C + f
                    ffn_up(c, G, g, f)
                    if f == 0:
                        if not first:
                            ffn_down(c - 2, G - 1, FC - 2)
                        if do_kv:
                            sum_kv(H - 1, 0, g == 1, False)
                    if f == 1 and not first:
                        ffn_down(c - 2, G - 1, FC - 1)
                    if f == 2:
                        if do_kv:
                            sum_kv(H - 1, 1, False, g == 0)
                        if do_b:
                            if do_kv:
                                pe.wait_ge(k_s, TPG * H)
                            transpose_q(J)
                        ffn_down(c - 2, G, f - 2)
                    if f == 3:
                        if do_b:
                            if do_kv:
                                pe.wait_ge(vlo_s, 2 * H)
                            attention_out(J, bj)
                        ffn_down(c - 2, G, f - 2)
                    if f == 4:
                        if g == 0 and not is_last(b):
                            if do_b:
                                pe.wait_ge(x1_s, 2 * J + 1)
                            turn_kv(b + 1)
                        if do_a:
                            transpose_a(H, G)
                        ffn_down(c - 2, G, f - 2)
                    if f == 5:
                        if g == 0 and not is_last(b):
                            m_products(b + 1)
                        if do_a:
                            pe.wait_ge(qk_rows_in, 16 * (b + LEAD) + 16)
                            pe.wait_ge(hT_lo_s, 2 * H + 2)
                            if g == 0:
                                pe.wait_ge(mg_s, b + 2)
                            project(H, 0, b + LEAD)
                            project(H, 1, b + LEAD)
                        ffn_down(c - 2, G, f - 2)
                    if f == 6:
                        ffn_down(c - 2, G, f - 2)
                        if do_b:
                            if do_a:
                                pe.wait_ge(k_s, TPG * H + 2)
                            transpose_h(J)
                    if f == 7:
                        ffn_down(c - 2, G, f - 2)
                        if do_a:
                            pe.wait_ge(h2_lo_s, 2 * J + 2)
                            pe.wait_ge(vlo_s, 2 * H + 1)
                            project(H, 2, b + LEAD)
                            project(H, 3, b + LEAD)

            pe.wait_ge(w1_lo_s, 1)
            pe.wait_ge(w2_lo_s, 1)
            windows(pe, window)
            ffn_down(GROUPS * FC - 2, GROUPS - 1, FC - 2)
            ffn_down(GROUPS * FC - 1, GROUPS - 1, FC - 1)


_INS = ["L0_attn_x", "L0_attn_Wq", "L0_attn_bq", "L0_attn_Wk", "L0_attn_bk", "L0_attn_Wv", "L0_attn_bv",
        "L0_attn_Wo", "L0_attn_bo", "L0_ffn_W1", "L0_ffn_b1", "L0_ffn_quantum_phases",
        "L0_ffn_quantum_weights_real", "L0_ffn_quantum_weights_imag", "L0_ffn_W2", "L0_ffn_b2",
        "L0_c", "L0_wmod"]


def kernel(**inputs):
    import numpy as _np
    import concourse.bacc as _bacc
    from concourse import mybir as _mybir
    from concourse.bass_utils import run_bass_kernel_spmd as _run

    nc = _bacc.Bacc("TRN2", target_bir_lowering=False, num_devices=1)
    arrays, args = {}, []
    for name in _INS:
        a = _np.ascontiguousarray(inputs[name])
        arrays[f"in_{name}"] = a
        args.append(nc.dram_tensor(f"in_{name}", a.shape, _mybir.dt.from_np(a.dtype), kind="ExternalInput").ap())
    args.append(nc.dram_tensor("out", (BATCH, SEQ, D), _mybir.dt.float32, kind="ExternalOutput").ap())
    adaln_block(nc, *args)
    r = _run(nc, [arrays], core_ids=[0])
    return r.results[0]["out"]
```

```python
import math
from contextlib import ExitStack

import concourse.bass as bass
from concourse import mybir

F32 = mybir.dt.float32
F32R = mybir.dt.float32r
I32 = mybir.dt.int32
ALU = mybir.AluOpType
ACT = mybir.ActivationFunctionType
AX = mybir.AxisListType

P = 128
BATCH, SEQ, D = 8, 1024, 256
HD = 16
F = 1024
ROWS = SEQ // P
TPG = 4
GPB = ROWS // TPG
N = TPG * P
GROUPS = BATCH * GPB
DC = D // P
FC = F // P
QK, QKV = 2 * D, 3 * D
NH = D // HD
LN_EPS, ATT_EPS = 1e-5, 1e-6
TURN = 2 * math.pi
SIN_SCALE = 6.28318500518798828125
TURN_HI = 6.28125
TURN_LO = TURN - TURN_HI
ROUND = 1.5 * 2 ** 23
CONSTS = 7
AHEAD = 4
XR = 4


def adaln_block(nc, x, Wq, bq, Wk, bk, Wv, bv, Wo, bo, W1, b1, theta, w_re, w_im, W2, b2, c, wmod, out):
    x_v = x.rearrange("b (p t) d -> b p t d", p=P)
    out_v = out.rearrange("b (p t) d -> b p t d", p=P)

    split_rows = nc.dram_tensor("split_rows", (BATCH, 2, QK + 2 * D), F32, kind="Internal").ap()
    full_rows = nc.dram_tensor("full_rows", (BATCH, 3, D), F32, kind="Internal").ap()

    ctx = ExitStack()
    with ctx:
        def sb(name, shape, dt=F32):
            return ctx.enter_context(nc.sbuf_tensor(name, shape, dt))

        def pb(name):
            return ctx.enter_context(nc.psum_tensor(name, [P, 512], F32))

        xr = sb("xr", [P, XR, ROWS, D])
        q_ring = sb("q_ring", [P, 2, ROWS, D])
        wqkv_hi, wqkv_lo = (sb(f"wqkv_{s}", [P, DC, QKV], F32R) for s in ("hi", "lo"))
        w1_hi, w1_lo = (sb(f"w1_{s}", [P, DC, F], F32R) for s in ("hi", "lo"))
        w2_hi, w2_lo = (sb(f"w2_{s}", [P, FC, D], F32R) for s in ("hi", "lo"))
        wo_sb = sb("wo_sb", [P, DC, D])
        stage = sb("stage", [P, 2048])
        ident = sb("ident", [P, P])
        ones = sb("ones", [P, P])
        mask = sb("mask", [P, P])
        ones2 = sb("ones2", [2, P], F32R)
        b2_rows = sb("b2_rows", [2, 2 * D], F32R)
        CW = 2 * FC + 2 * DC
        cst = sb("cst", [P, BATCH, CW])
        cur_f = sb("cur_f", [P, 2, 2 * FC])
        cur_a = sb("cur_a", [P, 2, DC])
        cur_b = sb("cur_b", [P, 2, DC])
        gcoef = sb("gcoef", [P, FC])
        expo = sb("expo", [P, TPG])
        qk_rows = sb("qk_rows", [2, QK], F32R)
        o_rows = sb("o_rows", [2, 2 * D], F32R)
        ga_b, gb_b, bv_b = sb("ga_b", [P, D]), sb("gb_b", [P, D]), sb("bv_b", [P, D])
        st_a = sb("st_a", [P, TPG, 6])
        mv_a = sb("mv_a", [P, TPG, 2])
        ve_a = sb("ve_a", [P, TPG])
        rs_a = sb("rs_a", [P, TPG])
        xn_a = sb("xn_a", [P, TPG, D])
        hT_hi, hT_lo = sb("hT_hi", [P, DC, N], F32R), sb("hT_lo", [P, DC, N], F32R)
        er = sb("er", [P, TPG, QK])
        kf = sb("kf", [P, TPG, D])
        VW = P + 2
        v_sb = sb("v_sb", [P, TPG, DC, VW])
        kvm = sb("kvm", [P, DC, P])
        kvx = sb("kvx", [P, DC, P])
        ksr = sb("ksr", [P, DC, P])
        kvT_ks = sb("kvT_ks", [P, 2 * D])
        mg = sb("mg", [P, 2 * D])
        qp = sb("qp", [P, TPG, D])
        nrm = sb("nrm", [P, TPG * NH])
        nre = sb("nre", [P, TPG * NH])
        rno = sb("rno", [P, TPG * NH])
        qT = sb("qT", [P, DC, N])
        st_b = sb("st_b", [P, TPG, 6])
        mv_b = sb("mv_b", [P, TPG, 2])
        ve_b = sb("ve_b", [P, TPG])
        rs_b = sb("rs_b", [P, TPG])
        xn_b = sb("xn_b", [P, TPG, D])
        h2_hi, h2_lo = sb("h2_hi", [P, 2, DC, N], F32R), sb("h2_lo", [P, 2, DC, N], F32R)
        wk = sb("wk", [P, 4, N])
        nt = sb("nt", [P, 2, N])
        a_hi, a_lo = sb("a_hi", [P, 2, N], F32R), sb("a_lo", [P, 2, N], F32R)
        zv = sb("zv", [P, TPG, D])
        cT = sb("cT", [P, DC, BATCH])
        ce = sb("ce", [P, DC, BATCH])
        cr = sb("cr", [P, DC, BATCH])
        csil = sb("csil", [P, DC, BATCH])
        modT = sb("modT", [P, 4, DC, BATCH])
        th = sb("th", [P, 12, FC])
        thi = sb("thi", [P, FC], I32)

        U = [pb("U0"), pb("U1")]
        Y = [pb("Y0"), pb("Y1")]
        KV, V = pb("KV"), pb("V")
        Q = [pb("Q0"), pb("Q1")]

        wm = q_ring[:, :, :, :].rearrange("p a t d -> p (a t d)")[:, 0:DC * 6 * D] \
            .rearrange("p (k n) -> p k n", k=DC)
        xn_rows = xn_b[0:BATCH, :, :].rearrange("p t d -> p (t d)")
        bias8, bo8 = xn_rows[:, 0:QKV], xn_rows[:, QKV:QKV + D]
        full8 = zv[0:BATCH, :, :].rearrange("p t d -> p (t d)")[:, 0:3 * D]
        sp_hi, sp_lo = a_hi[0:BATCH, :, :].rearrange("p a n -> p (a n)"), \
            a_lo[0:BATCH, :, :].rearrange("p a n -> p (a n)")
        g8, neg8, mag8, go8 = wk[0:BATCH, 0, :], wk[0:BATCH, 1, :], wk[0:BATCH, 2, :], wk[0:BATCH, 3, 0:2 * D]
        qk8 = nt[0:BATCH, 0, :]
        b2f = kf[0:2, 0:2, :].rearrange("p t d -> p (t d)")
        c8, th_rows = xn_a[0:BATCH, 0, :], xn_a[0:4 * FC, 1, 0:P]
        b2h = sb("b2h", [2, 2 * D], F32R)
        stage_qkv = stage[:, 0:DC * QKV].rearrange("p (k n) -> p k n", k=DC)
        stage_w1 = stage[:, :].rearrange("p (k n) -> p k n", k=DC)
        stage_w2 = stage[:, :].rearrange("p (k n) -> p k n", k=FC)

        def sem(name):
            return ctx.enter_context(nc.semaphore(name))

        ld_c, ld_wm, ld_qkv, ld_rows, ld_th, ld_wo, ld_w1, ld_w2, ld_b2 = (
            sem(n) for n in ("ld_c", "ld_wm", "ld_qkv", "ld_rows", "ld_th", "ld_wo", "ld_w1", "ld_w2", "ld_b2"))
        rows_out = sem("rows_out")
        consts, dve_link = sem("consts"), sem("dve_link")
        turned, ce_s, silu_s, mod_mm, modT_s, trig_s = (sem(n) for n in ("turned", "ce_s", "silu_s", "mod_mm", "modT_s", "trig_s"))
        bias_mm, b1_mm, rows_s, b2hi_s, spl_s = (sem(n) for n in ("bias_mm", "b1_mm", "rows_s", "b2hi_s", "spl_s"))
        fixed_s, cst_s, wqkv_hi_s, wqkv_lo_s, w1_hi_s, w1_lo_s, w2_hi_s, w2_lo_s = (
            sem(n) for n in ("fixed_s", "cst_s", "wqkv_hi_s", "wqkv_lo_s", "w1_hi_s", "w1_lo_s", "w2_hi_s", "w2_lo_s"))
        x_in, x_out0, x_out1 = sem("x_in"), sem("x_out0"), sem("x_out1")
        qk_rows_in, o_rows_in, prep_rows_in, gb_in = (
            sem(n) for n in ("qk_rows_in", "o_rows_in", "prep_rows_in", "gb_in"))
        cura_s, stat_a, aggr_a, ve_a_s, rs_a_s, xn_a_s = (
            sem(n) for n in ("cura_s", "stat_a", "aggr_a", "ve_a_s", "rs_a_s", "xn_a_s"))
        tr_a, hT_hi_s, hT_lo_s = sem("tr_a"), sem("hT_hi_s"), sem("hT_lo_s")
        qk_mm, v_mm, relu_s, qpos_s, kpos_s, exp_s, q_s, k_s, v_s, kv_mm = (
            sem(n) for n in ("qk_mm", "v_mm", "relu_s", "qpos_s", "kpos_s", "exp_s", "q_s", "k_s", "v_s", "kv_mm"))
        kv_rd, kv_ev, prep_tr, prep_cp, m_mm, mg_s = (
            sem(n) for n in ("kv_rd", "kv_ev", "prep_tr", "prep_cp", "m_mm", "mg_s"))
        q_mul, n_sum, n_eps, n_rec, q_sc = (sem(n) for n in ("q_mul", "n_sum", "n_eps", "n_rec", "q_sc"))
        tr_q, qT_s, o_mm, x1_s = (sem(n) for n in ("tr_q", "qT_s", "o_mm", "x1_s"))
        curb_s, stat_b, aggr_b, ve_b_s, rs_b_s, xn_b_s = (
            sem(n) for n in ("curb_s", "stat_b", "aggr_b", "ve_b_s", "rs_b_s", "xn_b_s"))
        tr_h, h2_hi_s, h2_lo_s = sem("tr_h"), sem("h2_hi_s"), sem("h2_lo_s")
        curf_s, f1_mm, y_s, rv_s, kr_s, fr_s, sn_s, t_s, tb_s, ahi_s, alo_s, f2_mm = (
            sem(n) for n in ("curf_s", "f1_mm", "y_s", "rv_s", "kr_s", "fr_s", "sn_s", "t_s", "tb_s", "ahi_s", "alo_s", "f2_mm"))
        z_s, y_out = sem("z_s"), sem("y_out")

        block = ctx.enter_context(nc.Block())

        LEAD = AHEAD // GPB
        LAST_KV = GROUPS - AHEAD

        def windows(eng, window):
            for g in range(GPB):
                window(0, g, True, True, g > 0)
            with eng.Fori(1, BATCH - LEAD) as b:
                for g in range(GPB):
                    window(b, g, True, True, True)
            for b in range(BATCH - LEAD, BATCH):
                for g in range(GPB):
                    G = b * GPB + g
                    window(b, g, False, G + 1 < GROUPS, G <= LAST_KV)

        def stand_wait(eng, held, s, value):
            if not isinstance(value, int):
                eng.reg_mov(held, value)
                eng.wait_ge(consts, CONSTS)
                eng.wait_ge(s, held)
            else:
                eng.wait_ge(s, value)

        def is_first(b, g):
            return isinstance(b, int) and b == 0 and g == 0

        def do_next(b, g):
            return not isinstance(b, int) or b * GPB + g + 2 < GROUPS

        def is_last(b):
            return isinstance(b, int) and b == BATCH - 1

        @block.sync
        def _(sp):
            sp.dma_start(wm, wmod.rearrange("(k p) n -> p k n", p=P)).then_inc(ld_wm, 16)
            sp.dma_start(xr[:, 0, :, :], x_v[0]).then_inc(x_in, 16)
            for i, w in enumerate((Wq, Wk, Wv)):
                sp.dma_start(stage_qkv[:, :, i * D:(i + 1) * D],
                             w.rearrange("(k p) n -> p k n", p=P)).then_inc(ld_qkv, 16)
            sp.dma_start(wo_sb[:, :, :], Wo.rearrange("(k p) n -> p k n", p=P)).then_inc(ld_wo, 16)
            for b in range(1, XR):
                sp.wait_ge(x_in, 16 * b)
                sp.dma_start(xr[:, b, :, :], x_v[b]).then_inc(x_in, 16)
            sp.wait_ge(rows_s, 3)
            sp.dma_start(split_rows[:, 0, :], sp_hi.bitcast(F32)).then_inc(rows_out, 16)
            sp.dma_start(split_rows[:, 1, :], sp_lo.bitcast(F32)).then_inc(rows_out, 16)
            sp.dma_start(full_rows.rearrange("b r d -> b (r d)"), full8).then_inc(rows_out, 16)
            sp.wait_ge(rows_out, 48)

            def load_qk_rows(b):
                sp.dma_start(qk_rows[:, :].bitcast(F32), split_rows[b, :, 0:QK]).then_inc(qk_rows_in, 16)

            def load_o_rows(b):
                sp.dma_start(o_rows[:, :].bitcast(F32), split_rows[b, :, QK:QK + 2 * D]).then_inc(o_rows_in, 16)

            def load_prep_rows(b):
                sp.dma_start(ga_b[:, :], full_rows[b, 0:1, :].broadcast_to([P, D])).then_inc(prep_rows_in, 16)
                sp.dma_start(bv_b[:, :], full_rows[b, 2:3, :].broadcast_to([P, D])).then_inc(prep_rows_in, 16)

            def load_gb(b):
                sp.dma_start(gb_b[:, :], full_rows[b, 1:2, :].broadcast_to([P, D])).then_inc(gb_in, 16)

            load_qk_rows(0)
            load_prep_rows(0)
            load_o_rows(0)
            load_gb(0)
            sp.wait_ge(wqkv_hi_s, 1)
            sp.wait_ge(wqkv_lo_s, 1)
            sp.wait_ge(bias_mm, 2)
            sp.dma_start(stage_w1, W1.rearrange("(k p) n -> p k n", p=P)).then_inc(ld_w1, 16)
            sp.wait_ge(w1_hi_s, 1)
            sp.wait_ge(w1_lo_s, 1)
            sp.wait_ge(b1_mm, 1)
            sp.dma_start(stage_w2, W2.rearrange("(k p) n -> p k n", p=P)).then_inc(ld_w2, 16)
            sp.wait_ge(qk_mm, TPG * GPB)
            load_qk_rows(1)
            sp.wait_ge(mg_s, 1)
            load_prep_rows(1)
            sp.wait_ge(qk_mm, 2 * TPG * GPB)
            load_qk_rows(2)

            def batch(b, left):
                G = b * GPB
                if left >= 1:
                    sp.wait_ge(o_mm, 2 * G + 4)
                    load_o_rows(b + 1)
                if left >= 2:
                    sp.wait_ge(mg_s, b + 2)
                    load_prep_rows(b + 2)
                sp.wait_ge(y_out, TPG * (G + 1))
                sp.dma_start(out_v[b, :, 0:TPG, :], xr[:, b % XR, 0:TPG, :]).then_inc(x_out0, 16)
                if left >= 3:
                    sp.wait_ge(qk_mm, TPG * (G + AHEAD + GPB))
                    load_qk_rows(b + 3)
                if left >= 1:
                    sp.wait_ge(z_s, 2 * G + 4)
                    load_gb(b + 1)
                sp.wait_ge(y_out, TPG * (G + 2))
                sp.dma_start(out_v[b, :, TPG:ROWS, :], xr[:, b % XR, TPG:ROWS, :]).then_inc(x_out1, 16)
                if left >= XR:
                    sp.wait_ge(x_out0, 16 * (b + 1))
                    sp.wait_ge(x_out1, 16 * (b + 1))
                    sp.wait_ge(x_in, 16 * (b + XR))
                    sp.dma_start(xr[:, b % XR, :, :], x_v[b + XR]).then_inc(x_in, 16)

            with sp.Fori(0, BATCH - XR) as b:
                batch(b, XR)
            for b in range(BATCH - XR, BATCH):
                batch(b, BATCH - 1 - b)
            sp.wait_ge(x_out0, 16 * BATCH)
            sp.wait_ge(x_out1, 16 * BATCH)

        @block.gpsimd
        def _(gp):
            held = gp.alloc_register("held")
            gp.dma_start(b2f, b2.rearrange("(o a n) -> o a n", o=1, a=1).broadcast_to([2, 2, D])).then_inc(ld_b2, 16)
            for i, v in enumerate((bq, bk, bv, bo)):
                gp.dma_start(xn_rows[:, i * D:(i + 1) * D],
                             v.rearrange("(o n) -> o n", o=1).broadcast_to([BATCH, D])).then_inc(ld_rows, 16)
            for i, v in enumerate((theta, w_re, w_im, b1)):
                gp.dma_start(th_rows[i * FC:(i + 1) * FC, :], v.rearrange("(f p) -> f p", p=P)).then_inc(ld_th, 16)
            made = [0]

            def make(i):
                made[0] += 1
                i.then_inc(consts, 1)
                gp.wait_ge(consts, made[0])

            make(gp.memset(ident[:, :], 0.0))
            make(gp.affine_select(out=ident[:, :], in_=ident[:, :], compare_op=ALU.not_equal, fill=1.0,
                                  base=0, pattern=[[-1, P]], channel_multiplier=1))
            make(gp.memset(ones[:, :], 1.0))
            make(gp.memset(expo[:, :], -0.5))
            make(gp.memset(mask[:, :], 1.0))
            heads = mask[:, :].rearrange("p (j e) -> p j e", e=HD)
            make(gp.affine_select(out=heads, in_=heads, compare_op=ALU.is_ge, fill=0.0, base=0,
                                  pattern=[[-HD, P // HD], [0, HD]], channel_multiplier=1))
            make(gp.affine_select(out=heads, in_=heads, compare_op=ALU.is_ge, fill=0.0, base=HD - 1,
                                  pattern=[[HD, P // HD], [0, HD]], channel_multiplier=-1))
            assert made[0] == CONSTS

            def rstd_a(H):
                stand_wait(gp, held, aggr_a, TPG * H + TPG)
                gp.tensor_scalar(ve_a[:, :], mv_a[:, :, 1], 1.0, LN_EPS, ALU.mult, ALU.add).then_inc(ve_a_s, 1)
                gp.wait_ge(ve_a_s, H + 1)
                gp.tensor_tensor(rs_a[:, :], ve_a[:, :], expo[:, :], ALU.pow).then_inc(rs_a_s, 1)

            def rstd_b(J):
                stand_wait(gp, held, aggr_b, TPG * J + TPG)
                gp.tensor_scalar(ve_b[:, :], mv_b[:, :, 1], 1.0, LN_EPS, ALU.mult, ALU.add).then_inc(ve_b_s, 1)
                gp.wait_ge(ve_b_s, J + 1)
                gp.tensor_tensor(rs_b[:, :], ve_b[:, :], expo[:, :], ALU.pow).then_inc(rs_b_s, 1)

            def add_exp_k(H):
                for pair in range(2):
                    t = slice(2 * pair, 2 * pair + 2)
                    gp.wait_ge(exp_s, TPG * H + 2 * pair + 2)
                    gp.wait_ge(kpos_s, TPG * H + 2 * pair + 2)
                    gp.tensor_tensor(kf[:, t, :], kf[:, t, :], er[:, t, D:QK], ALU.add).then_inc(k_s, 1)

            def add_exp_q(H, b, g):
                for pair in range(2):
                    t = slice(2 * pair, 2 * pair + 2)
                    place = q_ring[:, b % 2, g * TPG + 2 * pair:g * TPG + 2 * pair + 2, :]
                    stand_wait(gp, held, qpos_s, TPG * H + 2 * pair + 2)
                    gp.tensor_tensor(place, place, er[:, t, 0:D], ALU.add).then_inc(q_s, 1)

            def q_times_ksum(J, b, g):
                stand_wait(gp, held, q_s, 2 * J + 2)
                stand_wait(gp, held, prep_cp, b + 1)
                if not (isinstance(J, int) and J == 0):
                    stand_wait(gp, held, tr_q, 2 * J)
                for t in range(TPG):
                    gp.tensor_tensor(qp[:, t, :], q_ring[:, b % 2, g * TPG + t, :],
                                     kvT_ks[:, D:2 * D], ALU.mult).then_inc(q_mul, 1)

            def q_scale(J, b, g):
                stand_wait(gp, held, n_rec, J + 1)
                for t in range(TPG):
                    gp.tensor_tensor(qp[:, t, :].rearrange("p (h e) -> p h e", e=HD),
                                     q_ring[:, b % 2, g * TPG + t, :].rearrange("p (h e) -> p h e", e=HD),
                                     rno[:, t * NH:(t + 1) * NH].unsqueeze(2).broadcast_to([P, NH, HD]),
                                     ALU.mult).then_inc(q_sc, 1)

            def fraction(c, f):
                gp.wait_ge(kr_s, c + 1)
                gp.tensor_tensor(wk[:, f % 4, :], wk[:, f % 4, :], nt[:, f % 2, :], ALU.subtract).then_inc(fr_s, 1)

            def add_bias(c, g, f):
                stand_wait(gp, held, t_s, c + 1)
                gp.tensor_scalar(wk[:, f % 4, :], wk[:, f % 4, :], 1.0, cur_f[:, g, FC + f:FC + f + 1],
                                 ALU.mult, ALU.add).then_inc(tb_s, 1)

            def residual(G, b, g):
                stand_wait(gp, held, z_s, 2 * G + 2)
                for t in range(TPG):
                    place = xr[:, b % XR, g * TPG + t, :]
                    gp.tensor_tensor(place, zv[:, t, :], place, ALU.add).then_inc(y_out, 1)

            for H in range(AHEAD):
                rstd_a(H)
                add_exp_k(H)
                add_exp_q(H, H // GPB, H % GPB)
            q_times_ksum(0, 0, 0)
            q_scale(0, 0, 0)
            rstd_b(0)
            q_times_ksum(1, 0, 1)
            q_scale(1, 0, 1)

            def window(b, g, do_a, do_b, do_kv):
                G = b * GPB + g
                J, H, C = G + 1, G + AHEAD, G * FC
                bj, gj = (b, 1) if g == 0 else (b + 1, 0)
                first = is_first(b, g)
                for f in range(FC):
                    c = C + f
                    if f > 0:
                        add_bias(c - 1, g, f - 1)
                    elif not first:
                        add_bias(c - 1, 1 - g, FC - 1)
                    fraction(c, f)
                    if f == 1 and do_kv:
                        add_exp_k(H - 1)
                    if f == 0 and do_a:
                        rstd_a(H)
                    if f == 5 and do_kv:
                        add_exp_q(H - 1, b + LEAD - 1 if g == 0 else b + LEAD, 1 - g)
                    if f == 3 and do_b:
                        rstd_b(J)
                    if f == 4 and not first:
                        residual(G - 1, *((b, 0) if g else (b - 1, 1)))
                    if f == 6 and do_b and do_next(b, g):
                        q_times_ksum(J + 1, b + 1, g)
                    if f == 7 and do_b and do_next(b, g):
                        q_scale(J + 1, b + 1, g)

            windows(gp, window)
            add_bias(GROUPS * FC - 1, 1, FC - 1)
            residual(GROUPS - 1, BATCH - 1, 1)

        @block.scalar
        def _(act):
            act.dma_start(c8, c).then_inc(ld_c, 16)
            act.wait_ge(turned, 1)
            act.activation(ce[:, :, :].rearrange("p k b -> p (k b)"), Y[0][:, 0:DC * BATCH], ACT.Exp,
                           scale=-1.0).then_inc(ce_s, 1)
            act.wait_ge(trig_s, 2)
            act.activation(th[:, 8:10, :], th[:, 6:8, :], ACT.Sin, scale=SIN_SCALE).then_inc(trig_s, 1)
            act.wait_ge(ld_qkv, 48)
            act.activation(wqkv_hi[:, :, :], stage_qkv, ACT.Copy).then_inc(wqkv_hi_s, 1)
            act.wait_ge(ld_b2, 16)
            act.activation(b2h[:, :], b2f, ACT.Copy).then_inc(b2hi_s, 1)

            def hT_high(H, ch, g):
                act.wait_ge(tr_a, 2 * H + ch + 1)
                if ch == 0:
                    act.wait_ge(cura_s, H + 1)
                act.activation(hT_hi[:, ch, :], Q[ch][:, :], ACT.Identity,
                               scale=cur_a[:, g, ch:ch + 1]).then_inc(hT_hi_s, 1)

            def negative_part(H, t):
                act.wait_ge(qk_mm, TPG * H + t + 1)
                if t == 0 and not (isinstance(H, int) and H == 0):
                    act.wait_ge(q_s, 2 * H)
                    act.wait_ge(k_s, 2 * H)
                act.activation(er[:, t, :], Q[t % 2][:, :], ACT.Relu, scale=-1.0).then_inc(relu_s, 1)

            def exps(H, pair):
                act.wait_ge(relu_s, TPG * H + 2 * pair + 2)
                for t in (2 * pair, 2 * pair + 1):
                    act.activation(er[:, t, :], er[:, t, :], ACT.Exp, scale=-1.0).then_inc(exp_s, 1)

            def copy_v(H, pair):
                first = isinstance(H, int) and H == 0
                act.wait_ge(v_mm, 2 * H + pair + 1)
                if pair == 0:
                    if first:
                        act.wait_ge(fixed_s, 2)
                    else:
                        act.wait_ge(kv_mm, 2 * H)
                act.activation(v_sb[:, 2 * pair:2 * pair + 2, :, 0:P],
                               V[:, :].rearrange("p (t h e) -> p t h e", t=2, h=DC), ACT.Copy).then_inc(v_s, 1)

            def copy_prep(b, J):
                act.wait_ge(prep_tr, b + 1)
                if J is not None:
                    act.wait_ge(q_mul, TPG * J + TPG)
                act.activation(kvT_ks[:, :], KV[:, :], ACT.Copy).then_inc(prep_cp, 1)

            def copy_qT(J, ch):
                act.wait_ge(tr_q, 2 * J + ch + 1)
                act.activation(qT[:, ch, :], Q[ch][:, :], ACT.Copy).then_inc(qT_s, 1)

            def h2_high(J, ch, g):
                act.wait_ge(tr_h, 2 * J + ch + 1)
                act.wait_ge(curb_s, J + 1)
                act.activation(h2_hi[:, g, ch, :], Q[ch][:, :], ACT.Identity,
                               scale=cur_b[:, g, ch:ch + 1]).then_inc(h2_hi_s, 1)

            def whole_turns(c, f, few):
                act.wait_ge(y_s, c + 1)
                if not few:
                    act.wait_ge(fr_s, c - 1)
                act.activation(nt[:, f % 2, :], wk[:, f % 4, :], ACT.Copy, bias=ROUND).then_inc(rv_s, 1)
                act.wait_ge(rv_s, c + 1)
                act.activation(nt[:, f % 2, :], nt[:, f % 2, :], ACT.Copy, bias=-ROUND).then_inc(kr_s, 1)

            def sine(c, f):
                act.wait_ge(fr_s, c + 1)
                act.activation(wk[:, f % 4, :], wk[:, f % 4, :], ACT.Sin, scale=SIN_SCALE).then_inc(sn_s, 1)

            def act_high(c, f, few):
                act.wait_ge(tb_s, c + 1)
                if not few:
                    act.wait_ge(f2_mm, c - 1)
                act.activation(a_hi[:, f % 2, :], wk[:, f % 4, :], ACT.Relu).then_inc(ahi_s, 1)

            for H in range(AHEAD):
                hT_high(H, 0, H % 2)
                hT_high(H, 1, H % 2)
                negative_part(H, 0)
                negative_part(H, 1)
                copy_v(H, 0)
                negative_part(H, 2)
                negative_part(H, 3)
                exps(H, 0)
                exps(H, 1)
                copy_v(H, 1)
                if H == 0:
                    act.wait_ge(ld_w1, 16)
                    act.activation(w1_hi[:, :, :], stage_w1, ACT.Copy).then_inc(w1_hi_s, 1)
                if H == 1:
                    act.wait_ge(ld_w2, 16)
                    act.activation(w2_hi[:, :, :], stage_w2, ACT.Copy).then_inc(w2_hi_s, 1)
                if H == GPB - 1:
                    copy_prep(0, None)
            copy_qT(0, 0)
            copy_qT(0, 1)
            h2_high(0, 0, 0)
            h2_high(0, 1, 0)

            def window(b, g, do_a, do_b, do_kv):
                G = b * GPB + g
                J, H, C = G + 1, G + AHEAD, G * FC
                first = is_first(b, g)
                for f in range(FC):
                    c = C + f
                    if f == 0 and do_kv:
                        negative_part(H - 1, 3)
                        copy_v(H - 1, 1)
                    if f == 1 and do_kv:
                        exps(H - 1, 0)
                    if f == 5 and do_b:
                        h2_high(J, 0, 1 - g)
                        h2_high(J, 1, 1 - g)
                    if f == 6 and do_a:
                        negative_part(H, 0)
                    if f == 7 and do_a:
                        negative_part(H, 2)
                    whole_turns(c, f, first and f < 2)
                    if not (first and f == 0):
                        act_high(c - 1, (f - 1) % FC, first and f <= 2)
                    if f == 6 and do_a:
                        copy_v(H, 0)
                        negative_part(H, 1)
                    if f == 1 and do_kv:
                        exps(H - 1, 1)
                    if f == 3 and do_a:
                        hT_high(H, 0, g)
                        hT_high(H, 1, g)
                    sine(c, f)
                    if f == 0 and do_b:
                        copy_qT(J, 0)
                        copy_qT(J, 1)
                    if f == 5 and g == 0 and not is_last(b):
                        copy_prep(b + 1, J)

            windows(act, window)
            act_high(GROUPS * FC - 1, FC - 1, False)

        @block.vector
        def _(dve):
            held = dve.alloc_register("held")
            chain = [0]

            def link(i):
                chain[0] += 1
                i.then_inc(dve_link, 1)
                dve.wait_ge(dve_link, chain[0])

            dve.wait_ge(consts, CONSTS)
            dve.tensor_copy(ones2[:, :], ones[0:2, :]).then_inc(fixed_s, 1)
            dve.tensor_copy(v_sb[:, :, :, P:VW], ones[:, 0:16].rearrange("p (t h e) -> p t h e", t=TPG, h=DC)) \
                .then_inc(fixed_s, 1)
            dve.wait_ge(ce_s, 1)
            link(dve.tensor_copy(cT[:, :, :].rearrange("p k b -> p (k b)"), Y[0][:, 0:DC * BATCH]))
            link(dve.tensor_scalar(cr[:, :, :], ce[:, :, :], 1.0, None, ALU.add))
            link(dve.reciprocal(ce[:, :, :], cr[:, :, :]))
            dve.tensor_tensor(csil[:, :, :], cT[:, :, :], ce[:, :, :], ALU.mult).then_inc(silu_s, 1)
            dve.wait_ge(turned, 2)
            link(dve.tensor_copy(th[:, 0:4, :].rearrange("p v f -> p (v f)"), Y[1][:, 0:4 * FC]))
            link(dve.tensor_scalar(thi[:, :], th[:, 0, :], 1 / TURN, None, ALU.mult))
            link(dve.scalar_tensor_tensor(out=th[:, 4, :], in0=thi[:, :], scalar=-TURN_HI, in1=th[:, 0, :],
                                          op0=ALU.mult, op1=ALU.add))
            link(dve.scalar_tensor_tensor(out=th[:, 5, :], in0=thi[:, :], scalar=-TURN_LO, in1=th[:, 4, :],
                                          op0=ALU.mult, op1=ALU.add))
            link(dve.tensor_scalar(th[:, 10, :], th[:, 5, :], 1 / TURN, None, ALU.mult))
            link(dve.tensor_scalar(th[:, 11, :], th[:, 10, :], 0.25, None, ALU.add))
            for i in range(2):
                link(dve.tensor_copy(thi[:, :], th[:, 10 + i, :]))
                dve.tensor_tensor(th[:, 6 + i, :], th[:, 10 + i, :], thi[:, :], ALU.subtract).then_inc(trig_s, 1)
                dve.wait_ge(trig_s, i + 1)
            dve.wait_ge(trig_s, 3)
            link(dve.tensor_tensor(th[:, 10, :], th[:, 9, :], th[:, 1, :], ALU.mult))
            link(dve.tensor_tensor(th[:, 11, :], th[:, 8, :], th[:, 2, :], ALU.mult))
            link(dve.tensor_tensor(th[:, 0, :], th[:, 10, :], th[:, 11, :], ALU.add))
            link(dve.scalar_tensor_tensor(out=gcoef[:, :], in0=th[:, 0, :], scalar=0.1, in1=th[:, 2, :],
                                          op0=ALU.mult, op1=ALU.mult))
            dve.wait_ge(mod_mm, 2)
            dve.tensor_copy(modT[:, :, :, :].rearrange("p j k b -> p (j k b)"),
                            Q[1][:, 0:4 * DC * BATCH]).then_inc(modT_s, 1)
            link(dve.tensor_copy(g8, Q[0][0:BATCH, :]))
            link(dve.tensor_scalar(neg8, g8, -1.0, None, ALU.mult))
            link(dve.tensor_tensor(mag8, g8, neg8, ALU.max))
            link(dve.tensor_scalar(neg8, mag8, 0.25, None, ALU.max))
            link(dve.tensor_scalar(mag8, g8, 0.0, 2.0, ALU.is_ge, ALU.mult))
            link(dve.scalar_tensor_tensor(out=g8, in0=mag8, scalar=-1.0, in1=neg8, op0=ALU.add, op1=ALU.mult))
            link(dve.tensor_copy(full8[:, 0:2 * D], g8))
            dve.wait_ge(ld_rows, 64)
            for i in range(2):
                link(dve.tensor_tensor(go8[:, i * D:(i + 1) * D], g8[:, 0:D], bo8, ALU.mult))
            dve.wait_ge(bias_mm, 2)
            link(dve.tensor_tensor(qk8, Y[0][0:BATCH, :], bias8[:, 0:QK], ALU.add))
            dve.tensor_tensor(full8[:, 2 * D:3 * D], Y[1][0:BATCH, 0:D], bias8[:, QK:QKV], ALU.add) \
                .then_inc(rows_s, 1)
            link(dve.tensor_copy(sp_hi[:, 0:QK], qk8))
            link(dve.tensor_copy(sp_hi[:, QK:QK + 2 * D], go8))
            dve.tensor_tensor(sp_lo[:, 0:QK], qk8, sp_hi[:, 0:QK].bitcast(F32), ALU.subtract).then_inc(rows_s, 1)
            dve.tensor_tensor(sp_lo[:, QK:QK + 2 * D], go8, sp_hi[:, QK:QK + 2 * D].bitcast(F32),
                              ALU.subtract).then_inc(rows_s, 1)
            dve.wait_ge(wqkv_hi_s, 1)
            dve.tensor_tensor(wqkv_lo[:, :, :], stage_qkv, wqkv_hi[:, :, :].bitcast(F32), ALU.subtract) \
                .then_inc(wqkv_lo_s, 1)
            dve.wait_ge(modT_s, 1)
            for i, j in enumerate((1, 3)):
                link(dve.tensor_scalar(cst[:, :, 2 * FC + i * DC:2 * FC + (i + 1) * DC].rearrange("p b k -> p k b"),
                                       modT[:, j, :, :], 1.0, None, ALU.add))
            dve.wait_ge(b2hi_s, 1)
            link(dve.tensor_scalar(cr[0:2, 0, 0:1], ident[0:2, 1:2], -2.0, 1.0, ALU.mult, ALU.add))
            link(dve.tensor_scalar(zv[0:2, 3, :].unsqueeze(1).broadcast_to([2, 1, D])[:, 0, :],
                                   b2h[:, 0:D].bitcast(F32), cr[0:2, 0, 0:1], None, ALU.mult))
            for i in range(2):
                link(dve.scalar_tensor_tensor(out=b2_rows[:, i * D:(i + 1) * D], in0=b2f[:, i * D:(i + 1) * D],
                                              scalar=ident[0:2, 1:2], in1=zv[0:2, 3, :],
                                              op0=ALU.mult, op1=ALU.add))

            def stats_a(H, b, g):
                dve.tensor_copy(cur_a[:, g, :], cst[:, b, 2 * FC:2 * FC + DC]).then_inc(cura_s, 1)
                stand_wait(dve, held, x_in, 16 * b + 16)
                for t in range(TPG):
                    dve.bn_stats(st_a[:, t, :], xr[:, b % XR, g * TPG + t, :]).then_inc(stat_a, 1)
                stand_wait(dve, held, stat_a, TPG * H + TPG)
                for t in range(TPG):
                    dve.bn_aggr(mv_a[:, t, :], st_a[:, t, :]).then_inc(aggr_a, 1)

            def apply_a(H, b, g):
                dve.wait_ge(rs_a_s, H + 1)
                if not (isinstance(H, int) and H == 0):
                    dve.wait_ge(tr_a, 2 * H)
                for t in range(TPG):
                    dve.tensor_scalar(xn_a[:, t, :], xr[:, b % XR, g * TPG + t, :], mv_a[:, t, 0:1],
                                      rs_a[:, t:t + 1], ALU.subtract, ALU.mult).then_inc(xn_a_s, 1)

            def hT_low(H, ch, g):
                dve.wait_ge(hT_hi_s, 2 * H + ch + 1)
                dve.scalar_tensor_tensor(out=hT_lo[:, ch, :], in0=Q[ch][:, :], scalar=cur_a[:, g, ch:ch + 1],
                                         in1=hT_hi[:, ch, :].bitcast(F32), op0=ALU.mult,
                                         op1=ALU.subtract).then_inc(hT_lo_s, 1)

            def positive_part(H, t, b, g):
                dve.wait_ge(relu_s, TPG * H + t + 1)
                if t == 0 and not (isinstance(H, int) and H == 0):
                    dve.wait_ge(kv_mm, 2 * H)
                dve.tensor_scalar(q_ring[:, b % 2, g * TPG + t, :], Q[t % 2][:, 0:D], 0.0, None,
                                  ALU.max).then_inc(qpos_s, 1)
                dve.tensor_scalar(kf[:, t, :], Q[t % 2][:, D:QK], 0.0, None, ALU.max).then_inc(kpos_s, 1)

            def read_kv(b):
                dve.wait_ge(kv_mm, 2 * GPB * (b + 1))
                dve.wait_ge(prep_rows_in, 32 * b + 32)
                for h in range(DC):
                    dve.scalar_tensor_tensor(out=kvx[:, h, :], in0=bv_b[:, h * P:(h + 1) * P],
                                             scalar=KV[:, h * 256 + P:h * 256 + P + 1],
                                             in1=KV[:, h * 256:h * 256 + P],
                                             op0=ALU.mult, op1=ALU.add).then_inc(kv_rd, 1)
                    dve.tensor_scalar(ksr[:, h, :], ones[:, :], KV[:, h * 256 + P:h * 256 + P + 1], None,
                                      ALU.mult).then_inc(kv_rd, 1)
                dve.wait_ge(kv_rd, 4 * b + 4)
                for h in range(DC):
                    dve.tensor_tensor(kvm[:, h, :], kvx[:, h, :], mask[:, :], ALU.mult).then_inc(kv_ev, 1)

            def gate_m(b):
                dve.wait_ge(m_mm, b + 1)
                if not (isinstance(b, int) and b == 0):
                    dve.wait_ge(o_mm, 2 * GPB * b)
                dve.tensor_tensor(mg[:, :].rearrange("p (h n) -> p h n", h=DC),
                                  KV[:, :].rearrange("p (h n) -> p h n", h=DC),
                                  ga_b[:, :].unsqueeze(1).broadcast_to([P, DC, D]), ALU.mult).then_inc(mg_s, 1)

            def normaliser(J):
                dve.wait_ge(q_mul, TPG * J + TPG)
                dve.tensor_reduce(out=nrm[:, :], in_=qp[:, :, :].rearrange("p t (h e) -> p (t h) e", e=HD),
                                  axis=AX.X, op=ALU.add).then_inc(n_sum, 1)
                dve.wait_ge(n_sum, J + 1)
                dve.tensor_scalar(nre[:, :], nrm[:, :], ATT_EPS, None, ALU.add).then_inc(n_eps, 1)
                dve.wait_ge(n_eps, J + 1)
                dve.reciprocal(rno[:, :], nre[:, :]).then_inc(n_rec, 1)

            def add_x(J, pair, b, g):
                dve.wait_ge(o_mm, 2 * J + pair + 1)
                place = xr[:, b % XR, g * TPG + 2 * pair:g * TPG + 2 * pair + 2, :]
                dve.tensor_tensor(place, (Q[0], V)[pair][:, :].rearrange("p (t d) -> p t d", t=2), place,
                                  ALU.add).then_inc(x1_s, 1)

            def stats_b(J, b, g):
                dve.tensor_copy(cur_b[:, g, :], cst[:, b, 2 * FC + DC:CW]).then_inc(curb_s, 1)
                stand_wait(dve, held, x1_s, 2 * J + 2)
                for t in range(TPG):
                    dve.bn_stats(st_b[:, t, :], xr[:, b % XR, g * TPG + t, :]).then_inc(stat_b, 1)
                stand_wait(dve, held, stat_b, TPG * J + TPG)
                for t in range(TPG):
                    dve.bn_aggr(mv_b[:, t, :], st_b[:, t, :]).then_inc(aggr_b, 1)

            def apply_b(J, b, g):
                dve.wait_ge(rs_b_s, J + 1)
                if not (isinstance(J, int) and J == 0):
                    dve.wait_ge(tr_h, 2 * J)
                for t in range(TPG):
                    dve.tensor_scalar(xn_b[:, t, :], xr[:, b % XR, g * TPG + t, :], mv_b[:, t, 0:1],
                                      rs_b[:, t:t + 1], ALU.subtract, ALU.mult).then_inc(xn_b_s, 1)

            def h2_low(J, ch, g):
                dve.wait_ge(h2_hi_s, 2 * J + ch + 1)
                dve.scalar_tensor_tensor(out=h2_lo[:, g, ch, :], in0=Q[ch][:, :], scalar=cur_b[:, g, ch:ch + 1],
                                         in1=h2_hi[:, g, ch, :].bitcast(F32), op0=ALU.mult,
                                         op1=ALU.subtract).then_inc(h2_lo_s, 1)

            def turns(c, G, g, f):
                dve.wait_ge(f1_mm, c + 1)
                if f == 0:
                    dve.wait_ge(curf_s, G + 1)
                if not (isinstance(c, int) and c < 4):
                    dve.wait_ge(alo_s, c - 3)
                dve.tensor_scalar(wk[:, f % 4, :], U[f % 2][:, :], 0.1 / TURN, cur_f[:, g, f:f + 1],
                                  ALU.mult, ALU.add).then_inc(y_s, 1)

            def add_sine(c, f):
                dve.wait_ge(sn_s, c + 1)
                dve.scalar_tensor_tensor(out=wk[:, f % 4, :], in0=wk[:, f % 4, :], scalar=gcoef[:, f:f + 1], in1=U[f % 2][:, :],
                                         op0=ALU.mult, op1=ALU.add).then_inc(t_s, 1)

            def act_low(c, f):
                dve.wait_ge(ahi_s, c + 1)
                dve.scalar_tensor_tensor(out=a_lo[:, f % 2, :], in0=wk[:, f % 4, :], scalar=0.0,
                                         in1=a_hi[:, f % 2, :].bitcast(F32), op0=ALU.max,
                                         op1=ALU.subtract).then_inc(alo_s, 1)

            def gate_out(G, b):
                dve.wait_ge(f2_mm, FC * G + FC)
                dve.wait_ge(gb_in, 16 * b + 16)
                if not (isinstance(G, int) and G == 0):
                    dve.wait_ge(y_out, TPG * G)
                for p in range(2):
                    dve.tensor_tensor(zv[:, 2 * p:2 * p + 2, :], Y[p][:, :].rearrange("p (t d) -> p t d", t=2),
                                      gb_b[:, :].unsqueeze(1).broadcast_to([P, 2, D]),
                                      ALU.mult).then_inc(z_s, 1)

            def take_constants(G, b, g):
                dve.tensor_copy(cur_f[:, g, :], cst[:, b, 0:2 * FC]).then_inc(curf_s, 1)

            for H in range(AHEAD):
                b, g = H // GPB, H % GPB
                stats_a(H, b, g)
                apply_a(H, b, g)
                hT_low(H, 0, g)
                hT_low(H, 1, g)
                for t in range(TPG):
                    positive_part(H, t, b, g)
                if H == 0:
                    dve.wait_ge(w1_hi_s, 1)
                    dve.tensor_tensor(w1_lo[:, :, :], stage_w1, w1_hi[:, :, :].bitcast(F32), ALU.subtract) \
                        .then_inc(w1_lo_s, 1)
                if H == 1:
                    dve.wait_ge(b1_mm, 1)
                    link(dve.tensor_tensor(cst[:, :, FC:2 * FC].rearrange("p b f -> p f b"),
                                           U[0][:, 0:FC * BATCH].rearrange("p (f b) -> p f b", b=BATCH),
                                           th[:, 3, :].unsqueeze(2).broadcast_to([P, FC, BATCH]), ALU.add))
                    link(dve.scalar_tensor_tensor(out=cst[:, :, 0:FC], in0=cst[:, :, FC:2 * FC],
                                                  scalar=0.1 / TURN,
                                                  in1=th[:, 6, :].unsqueeze(1).broadcast_to([P, BATCH, FC]),
                                                  op0=ALU.mult, op1=ALU.add))
                    dve.wait_ge(w2_hi_s, 1)
                    dve.tensor_tensor(w2_lo[:, :, :], stage_w2, w2_hi[:, :, :].bitcast(F32), ALU.subtract) \
                        .then_inc(w2_lo_s, 1)
                if H == GPB - 1:
                    read_kv(0)
                    gate_m(0)
            normaliser(0)
            add_x(0, 0, 0, 0)
            add_x(0, 1, 0, 0)
            stats_b(0, 0, 0)
            apply_b(0, 0, 0)
            h2_low(0, 0, 0)
            h2_low(0, 1, 0)
            normaliser(1)
            take_constants(0, 0, 0)

            def window(b, g, do_a, do_b, do_kv):
                G = b * GPB + g
                J, H, C = G + 1, G + AHEAD, G * FC
                bj, gj = (b, 1) if g == 0 else (b + 1, 0)
                bh = b + LEAD
                before = (b, 0) if g else (b - 1, 1)
                first = is_first(b, g)
                for f in range(FC):
                    c = C + f
                    if f == 2 and do_b:
                        add_x(J, 0, bj, gj)
                    if f == 3 and do_b:
                        add_x(J, 1, bj, gj)
                    if not (first and f < 2):
                        act_low(c - 2, (f - 2) % FC)
                    if f == 4 and do_a:
                        hT_low(H, 0, g)
                        hT_low(H, 1, g)
                    if f == 5 and do_b:
                        h2_low(J, 0, 1 - g)
                        h2_low(J, 1, 1 - g)
                    turns(c, G, g, f)
                    if f == 4 and do_b:
                        apply_b(J, bj, gj)
                    if not (first and f == 0):
                        add_sine(c - 1, (f - 1) % FC)
                    if f == 0 and do_kv:
                        positive_part(H - 1, 3, b + LEAD - 1 if g == 0 else b + LEAD, 1 - g)
                    if f == 0 and do_a:
                        stats_a(H, bh, g)
                    if f == 1 and not first:
                        gate_out(G - 1, before[0])
                    if f == 1 and do_a:
                        apply_a(H, bh, g)
                    if f == 3 and do_b:
                        stats_b(J, bj, gj)
                    if f == 4 and g == 0 and not is_last(b):
                        read_kv(b + 1)
                    if f == 6 and do_a:
                        positive_part(H, 0, bh, g)
                        positive_part(H, 1, bh, g)
                    if f == 7 and do_b and do_next(b, g):
                        normaliser(J + 1)
                    if f == 7 and do_a:
                        positive_part(H, 2, bh, g)
                    if f == 7 and g == 0 and not is_last(b):
                        gate_m(b + 1)
                    if f == 7 and not (is_last(b) and g == 1):
                        take_constants(J, bj, gj)

            windows(dve, window)
            act_low(GROUPS * FC - 2, FC - 2)
            add_sine(GROUPS * FC - 1, FC - 1)
            act_low(GROUPS * FC - 1, FC - 1)
            gate_out(GROUPS - 1, BATCH - 1)

        @block.tensor
        def _(pe):
            def passes(out, a, b, first, last):
                pe.matmul(out, a[0], b[0], start=first, stop=False)
                pe.matmul(out, a[0], b[1], start=False, stop=False)
                return pe.matmul(out, a[1], b[0], start=False, stop=last)

            pe.wait_ge(consts, 2)
            pe.wait_ge(ld_c, 16)
            for k in range(DC):
                last = pe.transpose(Y[0][:, k * BATCH:(k + 1) * BATCH], c8[:, k * P:(k + 1) * P],
                                    ident[0:BATCH, 0:BATCH])
            last.then_inc(turned, 1)
            pe.wait_ge(ld_th, 64)
            pe.transpose(Y[1][:, 0:4 * FC], th_rows, ident[0:4 * FC, 0:4 * FC]).then_inc(turned, 1)
            pe.wait_ge(silu_s, 1)
            pe.wait_ge(ld_wm, 16)
            for i, off in enumerate((2 * D, 5 * D)):
                for k in range(DC):
                    last = pe.matmul(Q[0][0:BATCH, i * D:(i + 1) * D], csil[:, k, :], wm[:, k, off:off + D],
                                     start=(k == 0), stop=(k == DC - 1))
            last.then_inc(mod_mm, 1)
            for j, off in enumerate((0, D, 3 * D, 4 * D)):
                for ch in range(DC):
                    at = (j * DC + ch) * BATCH
                    for k in range(DC):
                        last = pe.matmul(Q[1][:, at:at + BATCH], wm[:, k, off + ch * P:off + (ch + 1) * P],
                                         csil[:, k, :], start=(k == 0), stop=(k == DC - 1))
            last.then_inc(mod_mm, 1)
            pe.wait_ge(modT_s, 1)
            pe.wait_ge(ld_qkv, 48)
            for i, (o, off, n) in enumerate(((Y[0], 0, QK), (Y[1], QK, D))):
                for k in range(DC):
                    last = pe.matmul(o[0:BATCH, 0:n], modT[:, 0, k, :], stage_qkv[:, k, off:off + n],
                                     start=(k == 0), stop=(k == DC - 1))
                last.then_inc(bias_mm, 1)

            def transpose_a(H):
                pe.wait_ge(xn_a_s, TPG * H + TPG)
                for ch in range(DC):
                    for t in range(TPG):
                        last = pe.transpose(Q[ch][:, t * P:(t + 1) * P], xn_a[:, t, ch * P:(ch + 1) * P], ident[:, :])
                    last.then_inc(tr_a, 1)

            def qk_bank_free(H, t):
                pe.wait_ge(kpos_s, TPG * H + t + 1)

            def project(H, t):
                sl = slice(t * P, (t + 1) * P)
                pe.matmul(Q[t % 2][:, :], ones2[:, :], qk_rows[:, :], start=True, stop=False)
                for k in range(DC):
                    last = passes(Q[t % 2][:, :], (hT_hi[:, k, sl], hT_lo[:, k, sl]),
                                  (wqkv_hi[:, k, 0:QK], wqkv_lo[:, k, 0:QK]), False, k == DC - 1)
                last.then_inc(qk_mm, 1)
                for k in range(DC):
                    last = passes(V[:, (t % 2) * D:(t % 2 + 1) * D], (hT_hi[:, k, sl], hT_lo[:, k, sl]),
                                  (wqkv_hi[:, k, QK:QKV], wqkv_lo[:, k, QK:QKV]),
                                  t % 2 == 0 and k == 0, t % 2 == 1 and k == DC - 1)
                if t % 2:
                    last.then_inc(v_mm, 1)

            def sum_kv(H, pair, start, stop):
                pe.wait_ge(k_s, 2 * H + pair + 1)
                pe.wait_ge(v_s, 2 * H + pair + 1)
                for t in (2 * pair, 2 * pair + 1):
                    for h in range(DC):
                        last = pe.matmul(KV[:, h * 256:h * 256 + VW], kf[:, t, h * P:(h + 1) * P],
                                         v_sb[:, t, h, :], start=start and t == 0 and h == 0,
                                         stop=stop and t == TPG - 1 and h == DC - 1)
                last.then_inc(kv_mm, 1)

            def turn_kv(b):
                pe.wait_ge(kv_ev, 2 * b + 2)
                for h in range(DC):
                    pe.transpose(KV[:, h * P:(h + 1) * P], kvm[:, h, :], ident[:, :])
                for h in range(DC):
                    last = pe.matmul(KV[:, D + h * P:D + (h + 1) * P], ksr[:, h, :], ident[:, :],
                                     start=True, stop=True)
                last.then_inc(prep_tr, 1)

            def m_products(b):
                pe.wait_ge(prep_cp, b + 1)
                if isinstance(b, int) and b == 0:
                    pe.wait_ge(ld_wo, 16)
                for h in range(DC):
                    last = pe.matmul(KV[:, h * D:(h + 1) * D], kvT_ks[:, h * P:(h + 1) * P], wo_sb[:, h, :],
                                     start=True, stop=True)
                last.then_inc(m_mm, 1)

            def transpose_q(J):
                pe.wait_ge(q_sc, TPG * J + TPG)
                for ch in range(DC):
                    for t in range(TPG):
                        last = pe.transpose(Q[ch][:, t * P:(t + 1) * P], qp[:, t, ch * P:(ch + 1) * P], ident[:, :])
                    last.then_inc(tr_q, 1)

            def attention_out(J, pair, b):
                if pair == 0:
                    pe.wait_ge(qT_s, 2 * J + 2)
                    pe.wait_ge(mg_s, b + 1)
                    pe.wait_ge(o_rows_in, 16 * b + 16)
                o = (Q[0], V)[pair]
                pe.matmul(o[:, :], ones2[:, :], o_rows[:, :], start=True, stop=False)
                for t in range(2):
                    sl = slice((2 * pair + t) * P, (2 * pair + t + 1) * P)
                    for k in range(DC):
                        last = pe.matmul(o[:, t * D:(t + 1) * D], qT[:, k, sl], mg[:, k * D:(k + 1) * D],
                                         start=False, stop=t == 1 and k == DC - 1)
                last.then_inc(o_mm, 1)

            def transpose_h(J):
                pe.wait_ge(xn_b_s, TPG * J + TPG)
                for ch in range(DC):
                    for t in range(TPG):
                        last = pe.transpose(Q[ch][:, t * P:(t + 1) * P], xn_b[:, t, ch * P:(ch + 1) * P], ident[:, :])
                    last.then_inc(tr_h, 1)

            def ffn_up(c, G, g, f):
                if f == 0:
                    pe.wait_ge(h2_lo_s, 2 * G + 2)
                if not (isinstance(c, int) and c < 2):
                    pe.wait_ge(t_s, c - 1)
                fs = slice(f * P, (f + 1) * P)
                for k in range(DC):
                    last = passes(U[f % 2][:, :], (w1_hi[:, k, fs], w1_lo[:, k, fs]),
                                  (h2_hi[:, g, k, :], h2_lo[:, g, k, :]), k == 0, k == DC - 1)
                last.then_inc(f1_mm, 1)

            def ffn_down(c, G, f):
                pe.wait_ge(alo_s, c + 1)
                if f == 0:
                    if not (isinstance(G, int) and G == 0):
                        pe.wait_ge(z_s, 2 * G)
                    for p in range(2):
                        pe.matmul(Y[p][:, :], ones2[:, :], b2_rows[:, :], start=True, stop=False)
                for t in range(TPG):
                    sl = slice(t * P, (t + 1) * P)
                    last = passes(Y[t // 2][:, (t % 2) * D:(t % 2 + 1) * D],
                                  (a_hi[:, f % 2, sl], a_lo[:, f % 2, sl]),
                                  (w2_hi[:, f, :], w2_lo[:, f, :]), False, f == FC - 1 and t % 2 == 1)
                last.then_inc(f2_mm, 1)

            pe.wait_ge(wqkv_lo_s, 1)
            for H in range(AHEAD):
                b, g = H // GPB, H % GPB
                if H:
                    qk_bank_free(H - 1, TPG - 1)
                transpose_a(H)
                pe.wait_ge(qk_rows_in, 16 * (b + 1))
                pe.wait_ge(hT_lo_s, 2 * H + 2)
                if H:
                    pe.wait_ge(v_s, 2 * H)
                project(H, 0)
                project(H, 1)
                if H == 0:
                    pe.wait_ge(ld_w1, 16)
                    for f in range(FC):
                        for k in range(DC):
                            last = pe.matmul(U[0][:, f * BATCH:(f + 1) * BATCH], stage_w1[:, k, f * P:(f + 1) * P],
                                             modT[:, 2, k, :], start=(k == 0), stop=(k == DC - 1))
                    last.then_inc(b1_mm, 1)
                qk_bank_free(H, 0)
                pe.wait_ge(v_s, 2 * H + 1)
                project(H, 2)
                qk_bank_free(H, 1)
                project(H, 3)
                if H == GPB:
                    pe.wait_ge(mg_s, 1)
                sum_kv(H, 0, g == 0, False)
                sum_kv(H, 1, False, g == 1)
                if H == GPB - 1:
                    turn_kv(0)
                    m_products(0)
            qk_bank_free(AHEAD - 1, TPG - 1)
            transpose_q(0)
            pe.wait_ge(v_s, 2 * AHEAD)
            attention_out(0, 0, 0)
            attention_out(0, 1, 0)
            pe.wait_ge(x1_s, 1)
            transpose_h(0)

            def window(b, g, do_a, do_b, do_kv):
                G = b * GPB + g
                J, H, C = G + 1, G + AHEAD, G * FC
                bj = b if g == 0 else b + 1
                first = is_first(b, g)
                for f in range(FC):
                    c = C + f
                    ffn_up(c, G, g, f)
                    if f == 2 and do_b:
                        if do_kv:
                            pe.wait_ge(v_s, 2 * H)
                        attention_out(J, 1, bj)
                    if f == 3 and do_kv:
                        if g == 1:
                            pe.wait_ge(mg_s, b + 2)
                        sum_kv(H - 1, 0, g == 1, False)
                        sum_kv(H - 1, 1, False, g == 0)
                    if f == 5 and g == 0 and not is_last(b):
                        turn_kv(b + 1)
                    if f == 6 and do_a:
                        project(H, 1)
                    if f == 6 and g == 0 and not is_last(b):
                        m_products(b + 1)
                    if not (first and f < 2):
                        ffn_down(c - 2, G - (f < 2), (f - 2) % FC)
                    if f == 0 and do_b:
                        if do_kv:
                            qk_bank_free(H - 1, TPG - 1)
                        transpose_q(J)
                    if f == 1 and do_b:
                        attention_out(J, 0, bj)
                    if f == 3 and do_a:
                        pe.wait_ge(x1_s, 2 * J + 1)
                        transpose_a(H)
                    if f == 4 and do_b:
                        if do_a:
                            pe.wait_ge(hT_lo_s, 2 * H + 2)
                        transpose_h(J)
                    if f == 5 and do_a:
                        pe.wait_ge(qk_rows_in, 16 * (b + LEAD) + 16)
                        pe.wait_ge(h2_lo_s, 2 * J + 2)
                        pe.wait_ge(x1_s, 2 * J + 2)
                        project(H, 0)
                    if f == 6 and do_a:
                        qk_bank_free(H, 0)
                        pe.wait_ge(v_s, 2 * H + 1)
                        project(H, 2)
                    if f == 7 and do_a:
                        qk_bank_free(H, 1)
                        project(H, 3)

            windows(pe, window)
            ffn_down(GROUPS * FC - 2, GROUPS - 1, FC - 2)
            ffn_down(GROUPS * FC - 1, GROUPS - 1, FC - 1)


_INS = ["L0_attn_x", "L0_attn_Wq", "L0_attn_bq", "L0_attn_Wk", "L0_attn_bk", "L0_attn_Wv", "L0_attn_bv",
        "L0_attn_Wo", "L0_attn_bo", "L0_ffn_W1", "L0_ffn_b1", "L0_ffn_quantum_phases",
        "L0_ffn_quantum_weights_real", "L0_ffn_quantum_weights_imag", "L0_ffn_W2", "L0_ffn_b2",
        "L0_c", "L0_wmod"]


def kernel(**inputs):
    import numpy as _np
    import concourse.bacc as _bacc
    from concourse import mybir as _mybir
    from concourse.bass_utils import run_bass_kernel_spmd as _run

    nc = _bacc.Bacc("TRN2", target_bir_lowering=False, num_devices=1)
    arrays, args = {}, []
    for name in _INS:
        a = _np.ascontiguousarray(inputs[name])
        arrays[f"in_{name}"] = a
        args.append(nc.dram_tensor(f"in_{name}", a.shape, _mybir.dt.from_np(a.dtype), kind="ExternalInput").ap())
    args.append(nc.dram_tensor("out", (BATCH, SEQ, D), _mybir.dt.float32, kind="ExternalOutput").ap())
    adaln_block(nc, *args)
    r = _run(nc, [arrays], core_ids=[0])
    return r.results[0]["out"]
```

```python
import math
from contextlib import ExitStack

import concourse.bass as bass
from concourse import mybir

F32 = mybir.dt.float32
F32R = mybir.dt.float32r
I32 = mybir.dt.int32
ALU = mybir.AluOpType
ACT = mybir.ActivationFunctionType
AX = mybir.AxisListType

P = 128
BATCH, SEQ, D = 8, 1024, 256
HD = 16
F = 1024
ROWS = SEQ // P
TPG = 4
GPB = ROWS // TPG
N = TPG * P
GROUPS = BATCH * GPB
DC = D // P
FC = F // P
QK, QKV = 2 * D, 3 * D
NH = D // HD
LN_EPS, ATT_EPS = 1e-5, 1e-6
TURN = 2 * math.pi
SIN_SCALE = 6.28318500518798828125
TURN_HI = 6.28125
TURN_LO = TURN - TURN_HI
ROUND = 1.5 * 2 ** 23
CONSTS = 7
AHEAD = 4
XR = 4


def adaln_block(nc, x, Wq, bq, Wk, bk, Wv, bv, Wo, bo, W1, b1, theta, w_re, w_im, W2, b2, c, wmod, out):
    x_v = x.rearrange("b (p t) d -> b p t d", p=P)
    out_v = out.rearrange("b (p t) d -> b p t d", p=P)

    split_rows = nc.dram_tensor("split_rows", (BATCH, 2, QK + 2 * D), F32, kind="Internal").ap()
    full_rows = nc.dram_tensor("full_rows", (BATCH, 3, D), F32, kind="Internal").ap()

    ctx = ExitStack()
    with ctx:
        def sb(name, shape, dt=F32):
            return ctx.enter_context(nc.sbuf_tensor(name, shape, dt))

        def pb(name):
            return ctx.enter_context(nc.psum_tensor(name, [P, 512], F32))

        xr = sb("xr", [P, XR, ROWS, D])
        q_ring = sb("q_ring", [P, 2, ROWS, D])
        wqkv_hi, wqkv_lo = (sb(f"wqkv_{s}", [P, DC, QKV], F32R) for s in ("hi", "lo"))
        w1_hi, w1_lo = (sb(f"w1_{s}", [P, DC, F], F32R) for s in ("hi", "lo"))
        w2_hi, w2_lo = (sb(f"w2_{s}", [P, FC, D], F32R) for s in ("hi", "lo"))
        wo_sb = sb("wo_sb", [P, DC, D])
        stage = sb("stage", [P, 2048])
        ident = sb("ident", [P, P])
        ones = sb("ones", [P, P])
        mask = sb("mask", [P, P])
        ones2 = sb("ones2", [2, P], F32R)
        b2_rows = sb("b2_rows", [2, 2 * D], F32R)
        CW = 2 * FC + 2 * DC
        cst = sb("cst", [P, BATCH, CW])
        cur_f = sb("cur_f", [P, 2, 2 * FC])
        cur_a = sb("cur_a", [P, 2, DC])
        cur_b = sb("cur_b", [P, 2, DC])
        gcoef = sb("gcoef", [P, FC])
        expo = sb("expo", [P, TPG])
        qk_rows = sb("qk_rows", [2, 2, QK], F32R)
        o_rows = sb("o_rows", [2, 2 * D], F32R)
        ga_b, gb_b, bv_b = sb("ga_b", [P, D]), sb("gb_b", [P, D]), sb("bv_b", [P, D])
        st_a = sb("st_a", [P, TPG, 6])
        mv_a = sb("mv_a", [P, TPG, 2])
        ve_a = sb("ve_a", [P, TPG])
        rs_a = sb("rs_a", [P, TPG])
        xn_a = sb("xn_a", [P, TPG, D])
        hT_hi, hT_lo = sb("hT_hi", [P, DC, N], F32R), sb("hT_lo", [P, DC, N], F32R)
        er = sb("er", [P, TPG, QK])
        kf = sb("kf", [P, TPG, D])
        VW = P + 2
        v_sb = sb("v_sb", [P, TPG, DC, VW])
        kvm = sb("kvm", [P, DC, P])
        kvx = sb("kvx", [P, DC, P])
        ksr = sb("ksr", [P, DC, P])
        kvT_ks = sb("kvT_ks", [P, 2 * D])
        mg = sb("mg", [P, 2 * D])
        qp = sb("qp", [P, TPG, D])
        nrm = sb("nrm", [P, TPG * NH])
        nre = sb("nre", [P, TPG * NH])
        rno = sb("rno", [P, TPG * NH])
        qT = sb("qT", [P, DC, N])
        st_b = sb("st_b", [P, TPG, 6])
        mv_b = sb("mv_b", [P, TPG, 2])
        ve_b = sb("ve_b", [P, TPG])
        rs_b = sb("rs_b", [P, TPG])
        xn_b = sb("xn_b", [P, TPG, D])
        h2_hi, h2_lo = sb("h2_hi", [P, 2, DC, N], F32R), sb("h2_lo", [P, 2, DC, N], F32R)
        wk = sb("wk", [P, 4, N])
        nt = sb("nt", [P, 2, N])
        a_hi, a_lo = sb("a_hi", [P, 2, N], F32R), sb("a_lo", [P, 2, N], F32R)
        zv = sb("zv", [P, TPG, D])
        cT = sb("cT", [P, DC, BATCH])
        ce = sb("ce", [P, DC, BATCH])
        cr = sb("cr", [P, DC, BATCH])
        csil = sb("csil", [P, DC, BATCH])
        modT = sb("modT", [P, 4, DC, BATCH])
        th = sb("th", [P, 12, FC])
        thi = sb("thi", [P, FC], I32)

        U = [pb("U0"), pb("U1")]
        Y = [pb("Y0"), pb("Y1")]
        KV, V = pb("KV"), pb("V")
        Q = [pb("Q0"), pb("Q1")]

        wm = q_ring[:, :, :, :].rearrange("p a t d -> p (a t d)")[:, 0:DC * 6 * D] \
            .rearrange("p (k n) -> p k n", k=DC)
        xn_rows = xn_b[0:BATCH, :, :].rearrange("p t d -> p (t d)")
        bias8, bo8 = xn_rows[:, 0:QKV], xn_rows[:, QKV:QKV + D]
        full8 = zv[0:BATCH, :, :].rearrange("p t d -> p (t d)")[:, 0:3 * D]
        sp_hi, sp_lo = a_hi[0:BATCH, :, :].rearrange("p a n -> p (a n)"), \
            a_lo[0:BATCH, :, :].rearrange("p a n -> p (a n)")
        g8, neg8, mag8, go8 = wk[0:BATCH, 0, :], wk[0:BATCH, 1, :], wk[0:BATCH, 2, :], wk[0:BATCH, 3, 0:2 * D]
        qk8 = nt[0:BATCH, 0, :]
        b2f = qp[0:2, 0:2, :].rearrange("p t d -> p (t d)")
        c8, th_rows = nt[0:BATCH, 1, 0:D], nt[0:4 * FC, 1, D:D + P]
        b2h = qk_rows[:, 1, :]
        stage_qkv = stage[:, 0:DC * QKV].rearrange("p (k n) -> p k n", k=DC)
        stage_w1 = stage[:, :].rearrange("p (k n) -> p k n", k=DC)
        stage_w2 = stage[:, :].rearrange("p (k n) -> p k n", k=FC)

        h_early = [(h2_hi[:, i, :, :], h2_lo[:, i, :, :]) for i in range(2)]
        hT = (hT_hi[:, :, :], hT_lo[:, :, :])

        def sem(name):
            return ctx.enter_context(nc.semaphore(name))

        ld_c, ld_wm, ld_qkv, ld_rows, ld_th, ld_wo, ld_w1, ld_w2, ld_b2 = (
            sem(n) for n in ("ld_c", "ld_wm", "ld_qkv", "ld_rows", "ld_th", "ld_wo", "ld_w1", "ld_w2", "ld_b2"))
        rows_out = sem("rows_out")
        consts, dve_link = sem("consts"), sem("dve_link")
        turned, ce_s, silu_s, mod_mm, modT_s, trig_s = (
            sem(n) for n in ("turned", "ce_s", "silu_s", "mod_mm", "modT_s", "trig_s"))
        bias_mm, b1_mm, rows_s, b2hi_s, b2_s = (sem(n) for n in ("bias_mm", "b1_mm", "rows_s", "b2hi_s", "b2_s"))
        fixed_s, wqkv_hi_s, wqkv_lo_s, w1_hi_s, w1_lo_s, w2_hi_s, w2_lo_s = (
            sem(n) for n in ("fixed_s", "wqkv_hi_s", "wqkv_lo_s", "w1_hi_s", "w1_lo_s", "w2_hi_s", "w2_lo_s"))
        x_in, x_out0, x_out1 = sem("x_in"), sem("x_out0"), sem("x_out1")
        qk_rows_in, o_rows_in, prep_rows_in, gb_in = (
            sem(n) for n in ("qk_rows_in", "o_rows_in", "prep_rows_in", "gb_in"))
        cura_s, stat_a, aggr_a, ve_a_s, rs_a_s, xn_a_s = (
            sem(n) for n in ("cura_s", "stat_a", "aggr_a", "ve_a_s", "rs_a_s", "xn_a_s"))
        tr_a, hT_hi_s, hT_lo_s = sem("tr_a"), sem("hT_hi_s"), sem("hT_lo_s")
        qk_mm, v_mm, relu_s, qpos_s, kpos_s, exp_s, q_s, k_s, v_s, kv_mm = (
            sem(n) for n in ("qk_mm", "v_mm", "relu_s", "qpos_s", "kpos_s", "exp_s", "q_s", "k_s", "v_s", "kv_mm"))
        kv_rd, kv_ev, prep_tr, prep_cp, m_mm, mg_s = (
            sem(n) for n in ("kv_rd", "kv_ev", "prep_tr", "prep_cp", "m_mm", "mg_s"))
        q_mul, n_sum, n_eps, n_rec, q_sc = (sem(n) for n in ("q_mul", "n_sum", "n_eps", "n_rec", "q_sc"))
        tr_q, qT_s, o_mm, x1_s = (sem(n) for n in ("tr_q", "qT_s", "o_mm", "x1_s"))
        curb_s, stat_b, aggr_b, ve_b_s, rs_b_s, xn_b_s = (
            sem(n) for n in ("curb_s", "stat_b", "aggr_b", "ve_b_s", "rs_b_s", "xn_b_s"))
        tr_h, h2_hi_s, h2_lo_s = sem("tr_h"), sem("h2_hi_s"), sem("h2_lo_s")
        curf_s, f1_mm, y_s, kr_s, fr_s, sn_s, t_s, tb_s, ahi_s, alo_s, f2_mm = (
            sem(n) for n in ("curf_s", "f1_mm", "y_s", "kr_s", "fr_s", "sn_s", "t_s", "tb_s", "ahi_s", "alo_s", "f2_mm"))
        z_s, y_out = sem("z_s"), sem("y_out")

        block = ctx.enter_context(nc.Block())

        LEAD = AHEAD // GPB
        LAST_KV = GROUPS - AHEAD

        def windows(eng, window):
            for g in range(GPB):
                window(0, g, True, True, True)
            with eng.Fori(1, BATCH - LEAD) as b:
                for g in range(GPB):
                    window(b, g, True, True, True)
            for b in range(BATCH - LEAD, BATCH):
                for g in range(GPB):
                    G = b * GPB + g
                    window(b, g, False, G + 1 < GROUPS, G <= LAST_KV)

        def stand_wait(eng, held, s, value):
            if not isinstance(value, int):
                eng.reg_mov(held, value)
                eng.wait_ge(consts, CONSTS)
                eng.wait_ge(s, held)
            else:
                eng.wait_ge(s, value)

        def is_first(b, g):
            return isinstance(b, int) and b == 0 and g == 0

        def times_ksum(eng, b, g):
            for t in range(TPG):
                eng.tensor_tensor(qp[:, t, :], q_ring[:, b % 2, g * TPG + t, :],
                                  kvT_ks[:, D:2 * D], ALU.mult).then_inc(q_mul, 1)

        def over_norm(eng, b, g):
            for t in range(TPG):
                eng.tensor_tensor(qp[:, t, :].rearrange("p (h e) -> p h e", e=HD),
                                  q_ring[:, b % 2, g * TPG + t, :].rearrange("p (h e) -> p h e", e=HD),
                                  rno[:, t * NH:(t + 1) * NH].unsqueeze(2).broadcast_to([P, NH, HD]),
                                  ALU.mult).then_inc(q_sc, 1)

        def do_next(b, g):
            return not isinstance(b, int) or b * GPB + g + 2 < GROUPS

        def is_last(b):
            return isinstance(b, int) and b == BATCH - 1

        @block.sync
        def _(sp):
            sp.dma_start(c8, c).then_inc(ld_c, 16)
            sp.dma_start(wm, wmod.rearrange("(k p) n -> p k n", p=P)).then_inc(ld_wm, 16)
            sp.dma_start(xr[:, 0, :, :], x_v[0]).then_inc(x_in, 16)
            for i, w in enumerate((Wq, Wk, Wv)):
                sp.dma_start(stage_qkv[:, :, i * D:(i + 1) * D],
                             w.rearrange("(k p) n -> p k n", p=P)).then_inc(ld_qkv, 16)
            sp.dma_start(wo_sb[:, :, :], Wo.rearrange("(k p) n -> p k n", p=P)).then_inc(ld_wo, 16)
            sp.wait_ge(rows_s, 2)
            sp.dma_start(split_rows[:, 0, 0:QK], sp_hi[:, 0:QK].bitcast(F32)).then_inc(rows_out, 16)
            sp.dma_start(split_rows[:, 1, 0:QK], sp_lo[:, 0:QK].bitcast(F32)).then_inc(rows_out, 16)

            def load_qk_rows(b):
                sp.dma_start(qk_rows[:, b % 2, :].bitcast(F32), split_rows[b, :, 0:QK]).then_inc(qk_rows_in, 16)

            def load_o_rows(b):
                sp.dma_start(o_rows[:, :].bitcast(F32), split_rows[b, :, QK:QK + 2 * D]).then_inc(o_rows_in, 16)

            def load_prep_rows(b):
                sp.dma_start(ga_b[:, :], full_rows[b, 0:1, :].broadcast_to([P, D])).then_inc(prep_rows_in, 16)
                sp.dma_start(bv_b[:, :], full_rows[b, 2:3, :].broadcast_to([P, D])).then_inc(prep_rows_in, 16)

            def load_gb(b):
                sp.dma_start(gb_b[:, :], full_rows[b, 1:2, :].broadcast_to([P, D])).then_inc(gb_in, 16)

            sp.wait_ge(wqkv_hi_s, 1)
            sp.wait_ge(wqkv_lo_s, 1)
            sp.wait_ge(bias_mm, 2)
            sp.dma_start(stage_w1, W1.rearrange("(k p) n -> p k n", p=P)).then_inc(ld_w1, 16)
            sp.wait_ge(x_in, 16)
            sp.dma_start(xr[:, 1, :, :], x_v[1]).then_inc(x_in, 16)
            sp.wait_ge(rows_s, 4)
            sp.dma_start(split_rows[:, 0, QK:QK + 2 * D], sp_hi[:, QK:QK + 2 * D].bitcast(F32)).then_inc(rows_out, 16)
            sp.dma_start(split_rows[:, 1, QK:QK + 2 * D], sp_lo[:, QK:QK + 2 * D].bitcast(F32)).then_inc(rows_out, 16)
            sp.dma_start(full_rows.rearrange("b r d -> b (r d)"), full8).then_inc(rows_out, 16)
            sp.wait_ge(b2_s, 2)
            sp.wait_ge(rows_out, 80)
            load_qk_rows(1)
            load_prep_rows(0)
            load_o_rows(0)
            load_gb(0)
            sp.wait_ge(w1_hi_s, 1)
            sp.wait_ge(w1_lo_s, 1)
            sp.wait_ge(b1_mm, 1)
            sp.dma_start(stage_w2, W2.rearrange("(k p) n -> p k n", p=P)).then_inc(ld_w2, 16)
            for b in range(2, XR):
                sp.wait_ge(x_in, 16 * b)
                sp.dma_start(xr[:, b, :, :], x_v[b]).then_inc(x_in, 16)
            sp.wait_ge(qk_rows_in, 16)
            load_qk_rows(2)
            sp.wait_ge(mg_s, 1)
            load_prep_rows(1)

            def batch(b, left):
                G = b * GPB
                if left >= 1:
                    sp.wait_ge(o_mm, 2 * G + 4)
                    load_o_rows(b + 1)
                if left >= 2:
                    sp.wait_ge(mg_s, b + 2)
                    load_prep_rows(b + 2)
                sp.wait_ge(y_out, TPG * (G + 1))
                sp.dma_start(out_v[b, :, 0:TPG, :], xr[:, b % XR, 0:TPG, :]).then_inc(x_out0, 16)
                if left >= 3:
                    sp.wait_ge(qk_rows_in, 16 * b + 32)
                    sp.wait_ge(qk_mm, TPG * (G + AHEAD))
                    load_qk_rows(b + 3)
                if left >= 1:
                    sp.wait_ge(z_s, 2 * G + 4)
                    load_gb(b + 1)
                sp.wait_ge(y_out, TPG * (G + 2))
                sp.dma_start(out_v[b, :, TPG:ROWS, :], xr[:, b % XR, TPG:ROWS, :]).then_inc(x_out1, 16)
                if left >= XR:
                    sp.wait_ge(x_out0, 16 * (b + 1))
                    sp.wait_ge(x_out1, 16 * (b + 1))
                    sp.wait_ge(x_in, 16 * (b + XR))
                    sp.dma_start(xr[:, b % XR, :, :], x_v[b + XR]).then_inc(x_in, 16)

            with sp.Fori(0, BATCH - XR) as b:
                batch(b, XR)
            for b in range(BATCH - XR, BATCH):
                batch(b, BATCH - 1 - b)
            sp.wait_ge(x_out0, 16 * BATCH)
            sp.wait_ge(x_out1, 16 * BATCH)

        @block.gpsimd
        def _(gp):
            held = gp.alloc_register("held")
            made = [0]

            def make(i):
                made[0] += 1
                i.then_inc(consts, 1)
                gp.wait_ge(consts, made[0])

            make(gp.memset(ident[:, :], 0.0))
            make(gp.affine_select(out=ident[:, :], in_=ident[:, :], compare_op=ALU.not_equal, fill=1.0,
                                  base=0, pattern=[[-1, P]], channel_multiplier=1))
            make(gp.memset(ones[:, :], 1.0))
            make(gp.memset(expo[:, :], -0.5))
            make(gp.memset(mask[:, :], 1.0))
            heads = mask[:, :].rearrange("p (j e) -> p j e", e=HD)
            make(gp.affine_select(out=heads, in_=heads, compare_op=ALU.is_ge, fill=0.0, base=0,
                                  pattern=[[-HD, P // HD], [0, HD]], channel_multiplier=1))
            make(gp.affine_select(out=heads, in_=heads, compare_op=ALU.is_ge, fill=0.0, base=HD - 1,
                                  pattern=[[HD, P // HD], [0, HD]], channel_multiplier=-1))
            assert made[0] == CONSTS

            def rstd_a(H):
                stand_wait(gp, held, aggr_a, TPG * H + TPG)
                gp.tensor_scalar(ve_a[:, :], mv_a[:, :, 1], 1.0, LN_EPS, ALU.mult, ALU.add).then_inc(ve_a_s, 1)
                gp.wait_ge(ve_a_s, H + 1)
                gp.tensor_tensor(rs_a[:, :], ve_a[:, :], expo[:, :], ALU.pow).then_inc(rs_a_s, 1)

            def rstd_b(J):
                stand_wait(gp, held, aggr_b, TPG * J + TPG)
                gp.tensor_scalar(ve_b[:, :], mv_b[:, :, 1], 1.0, LN_EPS, ALU.mult, ALU.add).then_inc(ve_b_s, 1)
                gp.wait_ge(ve_b_s, J + 1)
                gp.tensor_tensor(rs_b[:, :], ve_b[:, :], expo[:, :], ALU.pow).then_inc(rs_b_s, 1)

            def add_exp_k(H):
                for pair in range(2):
                    t = slice(2 * pair, 2 * pair + 2)
                    gp.wait_ge(exp_s, TPG * H + 2 * pair + 2)
                    gp.wait_ge(kpos_s, TPG * H + 2 * pair + 2)
                    gp.tensor_tensor(kf[:, t, :], kf[:, t, :], er[:, t, D:QK], ALU.add).then_inc(k_s, 1)

            def add_exp_q(H, b, g):
                for pair in range(2):
                    t = slice(2 * pair, 2 * pair + 2)
                    place = q_ring[:, b % 2, g * TPG + 2 * pair:g * TPG + 2 * pair + 2, :]
                    stand_wait(gp, held, qpos_s, TPG * H + 2 * pair + 2)
                    gp.tensor_tensor(place, place, er[:, t, 0:D], ALU.add).then_inc(q_s, 1)

            def q_times_ksum(J, b, g):
                stand_wait(gp, held, q_s, 2 * J + 2)
                stand_wait(gp, held, prep_cp, b + 1)
                stand_wait(gp, held, tr_q, 2 * J)
                times_ksum(gp, b, g)

            def q_scale(J, b, g):
                stand_wait(gp, held, n_rec, J + 1)
                over_norm(gp, b, g)

            def fraction(c, f):
                gp.wait_ge(kr_s, c + 1)
                gp.tensor_tensor(wk[:, f % 4, :], wk[:, f % 4, :], nt[:, f % 2, :], ALU.subtract).then_inc(fr_s, 1)

            def add_bias(c, g, f):
                stand_wait(gp, held, t_s, c + 1)
                gp.tensor_scalar(wk[:, f % 4, :], wk[:, f % 4, :], 1.0, cur_f[:, g, FC + f:FC + f + 1],
                                 ALU.mult, ALU.add).then_inc(tb_s, 1)

            def residual(G, b, g):
                stand_wait(gp, held, z_s, 2 * G + 2)
                for t in range(TPG):
                    place = xr[:, b % XR, g * TPG + t, :]
                    gp.tensor_tensor(place, zv[:, t, :], place, ALU.add).then_inc(y_out, 1)

            rstd_a(0)
            rstd_a(1)
            add_exp_k(0)
            add_exp_q(0, 0, 0)
            rstd_a(2)
            add_exp_k(1)
            add_exp_q(1, 0, 1)
            rstd_a(3)
            add_exp_k(2)
            add_exp_q(2, 1, 0)
            q_times_ksum(1, 0, 1)
            rstd_b(0)
            q_scale(1, 0, 1)

            def window(b, g, do_a, do_b, do_kv):
                G = b * GPB + g
                J, H, C = G + 1, G + AHEAD, G * FC
                bj, gj = (b, 1) if g == 0 else (b + 1, 0)
                first = is_first(b, g)
                late = int(not do_a)
                for f in range(FC):
                    c = C + f
                    if f == 3 and not first:
                        residual(G - 1, *((b, 0) if g else (b - 1, 1)))
                    fraction(c, f)
                    if f == 3 + late and do_b:
                        rstd_b(J)
                    if f == 1 and do_kv:
                        add_exp_k(H - 1)
                    if f > 0:
                        add_bias(c - 1, g, f - 1)
                    elif not first:
                        add_bias(c - 1, 1 - g, FC - 1)
                    if f == 7 and do_b and do_next(b, g):
                        q_scale(J + 1, b + 1, g)
                    if f == 0 and do_a:
                        rstd_a(H)
                    if f == 5 and do_b and do_next(b, g):
                        q_times_ksum(J + 1, b + 1, g)
                    if f == 4 and do_kv:
                        add_exp_q(H - 1, b + LEAD - 1 if g == 0 else b + LEAD, 1 - g)

            windows(gp, window)
            add_bias(GROUPS * FC - 1, 1, FC - 1)
            residual(GROUPS - 1, BATCH - 1, 1)

        @block.scalar
        def _(act):
            act.wait_ge(turned, 1)
            act.activation(ce[:, :, :].rearrange("p k b -> p (k b)"), Y[0][:, 0:DC * BATCH], ACT.Exp,
                           scale=-1.0).then_inc(ce_s, 1)
            for i, v in enumerate((theta, w_re, w_im, b1)):
                act.dma_start(th_rows[i * FC:(i + 1) * FC, :], v.rearrange("(f p) -> f p", p=P)).then_inc(ld_th, 16)
            for i, v in enumerate((bq, bk, bv, bo)):
                act.dma_start(xn_rows[:, i * D:(i + 1) * D],
                              v.rearrange("(o n) -> o n", o=1).broadcast_to([BATCH, D])).then_inc(ld_rows, 16)
            for i in range(2):
                act.dma_start(b2f[:, i * D:(i + 1) * D],
                              b2.rearrange("(o n) -> o n", o=1).broadcast_to([2, D])).then_inc(ld_b2, 16)
            act.wait_ge(ld_qkv, 48)
            act.activation(wqkv_hi[:, :, :], stage_qkv, ACT.Copy).then_inc(wqkv_hi_s, 1)

            def hT_high(H, ch, g, banks=Q, h=hT):
                act.wait_ge(tr_a, 2 * H + ch + 1)
                if ch == 0:
                    act.wait_ge(cura_s, H + 1)
                act.activation(h[0][:, ch, :], banks[ch][:, :], ACT.Identity,
                               scale=cur_a[:, g, ch:ch + 1]).then_inc(hT_hi_s, 1)

            def negative_part(H, t):
                act.wait_ge(qk_mm, TPG * H + t + 1)
                if t % 2 == 0 and not (isinstance(H, int) and H == 0):
                    act.wait_ge(q_s, 2 * H - 1 + t // 2)
                    act.wait_ge(k_s, 2 * H - 1 + t // 2)
                act.activation(er[:, t, :], Q[t % 2][:, :], ACT.Relu, scale=-1.0).then_inc(relu_s, 1)

            def exps(H, pair):
                act.wait_ge(relu_s, TPG * H + 2 * pair + 2)
                for t in (2 * pair, 2 * pair + 1):
                    act.activation(er[:, t, :], er[:, t, :], ACT.Exp, scale=-1.0).then_inc(exp_s, 1)

            def copy_v(H, pair):
                first = isinstance(H, int) and H == 0
                act.wait_ge(v_mm, 2 * H + pair + 1)
                if pair == 0:
                    if first:
                        act.wait_ge(fixed_s, 2)
                    else:
                        act.wait_ge(kv_mm, 2 * H)
                act.activation(v_sb[:, 2 * pair:2 * pair + 2, :, 0:P],
                               V[:, :].rearrange("p (t h e) -> p t h e", t=2, h=DC), ACT.Copy).then_inc(v_s, 1)

            def copy_prep(b, J):
                act.wait_ge(prep_tr, b + 1)
                if J is not None:
                    act.wait_ge(q_mul, TPG * J + TPG)
                act.activation(kvT_ks[:, :], KV[:, :], ACT.Copy).then_inc(prep_cp, 1)

            def copy_qT(J, ch, banks=Q):
                act.wait_ge(tr_q, 2 * J + ch + 1)
                act.activation(qT[:, ch, :], banks[ch][:, :], ACT.Copy).then_inc(qT_s, 1)

            def h2_high(J, ch, g, banks=Q):
                act.wait_ge(tr_h, 2 * J + ch + 1)
                act.wait_ge(curb_s, J + 1)
                act.activation(h2_hi[:, g, ch, :], banks[ch][:, :], ACT.Identity,
                               scale=cur_b[:, g, ch:ch + 1]).then_inc(h2_hi_s, 1)

            def turns(c, G, g, f):
                act.wait_ge(f1_mm, c + 1)
                if f == 0:
                    act.wait_ge(curf_s, G + 1)
                if not (isinstance(c, int) and c < 4):
                    act.wait_ge(alo_s, c - 3)
                act.activation(wk[:, f % 4, :], U[f % 2][:, :], ACT.Identity, scale=0.1 / TURN,
                               bias=cur_f[:, g, f:f + 1]).then_inc(y_s, 1)

            def sine(c, f):
                act.wait_ge(fr_s, c + 1)
                act.activation(wk[:, f % 4, :], wk[:, f % 4, :], ACT.Sin, scale=SIN_SCALE).then_inc(sn_s, 1)

            def act_high(c, f, few):
                act.wait_ge(tb_s, c + 1)
                if not few:
                    act.wait_ge(f2_mm, c - 1)
                act.activation(a_hi[:, f % 2, :], wk[:, f % 4, :], ACT.Relu).then_inc(ahi_s, 1)

            hT_high(0, 0, 0, U, h_early[0])
            hT_high(0, 1, 0, U, h_early[0])
            act.wait_ge(ld_b2, 32)
            act.activation(b2h, b2f, ACT.Copy).then_inc(b2hi_s, 1)
            for H in range(AHEAD):
                negative_part(H, 0)
                negative_part(H, 1)
                copy_v(H, 0)
                if H == 0:
                    act.wait_ge(ld_w1, 16)
                    act.activation(w1_hi[:, :, :], stage_w1, ACT.Copy).then_inc(w1_hi_s, 1)
                if H < AHEAD - 1:
                    hT_high(H + 1, 0, (H + 1) % 2, U, h_early[(H + 1) % 2])
                    hT_high(H + 1, 1, (H + 1) % 2, U, h_early[(H + 1) % 2])
                if H == GPB:
                    copy_prep(0, None)
                if H == AHEAD - 1:
                    copy_qT(0, 0, U)
                    copy_qT(0, 1, U)
                negative_part(H, 2)
                if H < AHEAD - 1:
                    negative_part(H, 3)
                    copy_v(H, 1)
                    exps(H, 0)
                    exps(H, 1)
                if H == GPB:
                    act.wait_ge(ld_w2, 16)
                    act.activation(w2_hi[:, :, :], stage_w2, ACT.Copy).then_inc(w2_hi_s, 1)
            act.wait_ge(trig_s, 2)
            act.activation(th[:, 8:10, :], th[:, 6:8, :], ACT.Sin, scale=SIN_SCALE).then_inc(trig_s, 1)
            h2_high(0, 0, 0, U)
            h2_high(0, 1, 0, U)

            def window(b, g, do_a, do_b, do_kv):
                G = b * GPB + g
                J, H, C = G + 1, G + AHEAD, G * FC
                first = is_first(b, g)
                late = int(not do_a)
                for f in range(FC):
                    c = C + f
                    if f == 0 and do_kv:
                        negative_part(H - 1, 3)
                    if f == 7 and do_a:
                        negative_part(H, 2)
                    turns(c, G, g, f)
                    if f == 1 and do_kv:
                        exps(H - 1, 0)
                    if not (first and f < 2):
                        act_high(c - 2, (f - 2) % FC, first and f < 4)
                    if f == 0 and do_kv:
                        copy_v(H - 1, 1)
                    if f == 6 and do_a:
                        negative_part(H, 1)
                    if f == 6 and do_a:
                        copy_v(H, 0)
                    if f == 1 and do_kv:
                        exps(H - 1, 1)
                    if f == 5 and do_a:
                        negative_part(H, 0)
                    if f == 3 and do_a:
                        hT_high(H, 0, g)
                        hT_high(H, 1, g)
                    if f == late and do_b:
                        copy_qT(J, 0)
                        copy_qT(J, 1)
                    if f == 4 + late and do_b:
                        h2_high(J, 0, 1 - g)
                        h2_high(J, 1, 1 - g)
                    sine(c, f)
                    if f == 5 and g == 0 and not is_last(b):
                        copy_prep(b + 1, J)

            windows(act, window)
            act_high(GROUPS * FC - 2, FC - 2, False)
            act_high(GROUPS * FC - 1, FC - 1, False)

        @block.vector
        def _(dve):
            held = dve.alloc_register("held")
            chain = [0]

            def link(i):
                chain[0] += 1
                i.then_inc(dve_link, 1)
                dve.wait_ge(dve_link, chain[0])

            def early_constants():
                dve.wait_ge(consts, CONSTS)
                dve.tensor_copy(ones2[:, :], ones[0:2, :]).then_inc(fixed_s, 1)
                dve.tensor_copy(v_sb[:, :, :, P:VW],
                                ones[:, 0:16].rearrange("p (t h e) -> p t h e", t=TPG, h=DC)).then_inc(fixed_s, 1)
                dve.wait_ge(ce_s, 1)
                link(dve.tensor_copy(cT[:, :, :].rearrange("p k b -> p (k b)"), Y[0][:, 0:DC * BATCH]))
                link(dve.tensor_scalar(cr[:, :, :], ce[:, :, :], 1.0, None, ALU.add))
                link(dve.reciprocal(ce[:, :, :], cr[:, :, :]))
                dve.tensor_tensor(csil[:, :, :], cT[:, :, :], ce[:, :, :], ALU.mult).then_inc(silu_s, 1)

            def theta_in_turns():
                dve.wait_ge(turned, 2)
                link(dve.tensor_copy(th[:, 0:4, :].rearrange("p v f -> p (v f)"), Y[1][:, 0:4 * FC]))
                link(dve.tensor_scalar(thi[:, :], th[:, 0, :], 1 / TURN, None, ALU.mult))
                link(dve.scalar_tensor_tensor(out=th[:, 4, :], in0=thi[:, :], scalar=-TURN_HI, in1=th[:, 0, :],
                                              op0=ALU.mult, op1=ALU.add))
                link(dve.scalar_tensor_tensor(out=th[:, 5, :], in0=thi[:, :], scalar=-TURN_LO, in1=th[:, 4, :],
                                              op0=ALU.mult, op1=ALU.add))
                link(dve.tensor_scalar(th[:, 10, :], th[:, 5, :], 1 / TURN, None, ALU.mult))
                link(dve.tensor_scalar(th[:, 11, :], th[:, 10, :], 0.25, None, ALU.add))
                for i in range(2):
                    link(dve.tensor_copy(thi[:, :], th[:, 10 + i, :]))
                    dve.tensor_tensor(th[:, 6 + i, :], th[:, 10 + i, :], thi[:, :], ALU.subtract).then_inc(trig_s, 1)
                    dve.wait_ge(trig_s, i + 1)

            def sine_factors():
                dve.wait_ge(trig_s, 3)
                link(dve.tensor_tensor(th[:, 10, :], th[:, 9, :], th[:, 1, :], ALU.mult))
                link(dve.tensor_tensor(th[:, 11, :], th[:, 8, :], th[:, 2, :], ALU.mult))
                link(dve.tensor_tensor(th[:, 0, :], th[:, 10, :], th[:, 11, :], ALU.add))
                link(dve.scalar_tensor_tensor(out=gcoef[:, :], in0=th[:, 0, :], scalar=0.1, in1=th[:, 2, :],
                                              op0=ALU.mult, op1=ALU.mult))

            def modulation():
                dve.wait_ge(mod_mm, 1)
                dve.tensor_copy(modT[:, :, :, :].rearrange("p j k b -> p (j k b)"),
                                Q[1][:, 0:4 * DC * BATCH]).then_inc(modT_s, 1)
                dve.wait_ge(modT_s, 1)
                for i, j in enumerate((1, 3)):
                    link(dve.tensor_scalar(cst[:, :, 2 * FC + i * DC:2 * FC + (i + 1) * DC].rearrange("p b k -> p k b"),
                                           modT[:, j, :, :], 1.0, None, ALU.add))

            def qkv_bias():
                dve.wait_ge(ld_rows, 64)
                dve.wait_ge(bias_mm, 2)
                link(dve.tensor_tensor(qk8, Y[0][0:BATCH, :], bias8[:, 0:QK], ALU.add))
                dve.tensor_tensor(full8[:, 2 * D:3 * D], Y[1][0:BATCH, 0:D], bias8[:, QK:QKV], ALU.add) \
                    .then_inc(rows_s, 1)
                link(dve.tensor_copy(sp_hi[:, 0:QK], qk8))
                dve.tensor_tensor(sp_lo[:, 0:QK], qk8, sp_hi[:, 0:QK].bitcast(F32), ALU.subtract).then_inc(rows_s, 1)

            def gates():
                dve.wait_ge(mod_mm, 2)
                link(dve.tensor_copy(g8, KV[0:BATCH, :]))
                link(dve.tensor_scalar(neg8, g8, -1.0, None, ALU.mult))
                link(dve.tensor_tensor(mag8, g8, neg8, ALU.max))
                link(dve.tensor_scalar(neg8, mag8, 0.25, None, ALU.max))
                link(dve.tensor_scalar(mag8, g8, 0.0, 2.0, ALU.is_ge, ALU.mult))
                link(dve.scalar_tensor_tensor(out=g8, in0=mag8, scalar=-1.0, in1=neg8, op0=ALU.add, op1=ALU.mult))
                dve.tensor_copy(full8[:, 0:2 * D], g8).then_inc(rows_s, 1)
                for i in range(2):
                    link(dve.tensor_tensor(go8[:, i * D:(i + 1) * D], g8[:, 0:D], bo8, ALU.mult))
                link(dve.tensor_copy(sp_hi[:, QK:QK + 2 * D], go8))
                dve.tensor_tensor(sp_lo[:, QK:QK + 2 * D], go8, sp_hi[:, QK:QK + 2 * D].bitcast(F32),
                                  ALU.subtract).then_inc(rows_s, 1)

            def rows_of_b2():
                dve.wait_ge(b2hi_s, 1)
                link(dve.tensor_scalar(cr[0:2, 0, 0:1], ident[0:2, 1:2], -2.0, 1.0, ALU.mult, ALU.add))
                link(dve.tensor_scalar(zv[0:2, 3, :], b2h[:, 0:D].bitcast(F32), cr[0:2, 0, 0:1], None, ALU.mult))
                for i in range(2):
                    dve.scalar_tensor_tensor(out=b2_rows[:, i * D:(i + 1) * D], in0=b2f[:, i * D:(i + 1) * D],
                                             scalar=ident[0:2, 1:2], in1=zv[0:2, 3, :],
                                             op0=ALU.mult, op1=ALU.add).then_inc(b2_s, 1)

            def ffn_bias():
                dve.wait_ge(b1_mm, 1)
                link(dve.tensor_tensor(cst[:, :, FC:2 * FC].rearrange("p b f -> p f b"),
                                       Y[0][:, 0:FC * BATCH].rearrange("p (f b) -> p f b", b=BATCH),
                                       th[:, 3, :].unsqueeze(2).broadcast_to([P, FC, BATCH]), ALU.add))
                link(dve.scalar_tensor_tensor(out=cst[:, :, 0:FC], in0=cst[:, :, FC:2 * FC],
                                              scalar=0.1 / TURN,
                                              in1=th[:, 6, :].unsqueeze(1).broadcast_to([P, BATCH, FC]),
                                              op0=ALU.mult, op1=ALU.add))

            def scale_a(b, g):
                dve.tensor_copy(cur_a[:, g, :], cst[:, b, 2 * FC:2 * FC + DC]).then_inc(cura_s, 1)

            def stats_a(H, b, g):
                stand_wait(dve, held, x_in, 16 * b + 16)
                for t in range(TPG):
                    dve.bn_stats(st_a[:, t, :], xr[:, b % XR, g * TPG + t, :]).then_inc(stat_a, 1)
                stand_wait(dve, held, stat_a, TPG * H + TPG)
                for t in range(TPG):
                    dve.bn_aggr(mv_a[:, t, :], st_a[:, t, :]).then_inc(aggr_a, 1)

            def apply_a(H, b, g):
                dve.wait_ge(rs_a_s, H + 1)
                if not (isinstance(H, int) and H == 0):
                    dve.wait_ge(tr_a, 2 * H)
                for t in range(TPG):
                    dve.tensor_scalar(xn_a[:, t, :], xr[:, b % XR, g * TPG + t, :], mv_a[:, t, 0:1],
                                      rs_a[:, t:t + 1], ALU.subtract, ALU.mult).then_inc(xn_a_s, 1)

            def hT_low(H, ch, g, banks=Q, h=hT):
                dve.wait_ge(hT_hi_s, 2 * H + ch + 1)
                dve.scalar_tensor_tensor(out=h[1][:, ch, :], in0=banks[ch][:, :], scalar=cur_a[:, g, ch:ch + 1],
                                         in1=h[0][:, ch, :].bitcast(F32), op0=ALU.mult,
                                         op1=ALU.subtract).then_inc(hT_lo_s, 1)

            def positive_part(H, t, b, g):
                dve.wait_ge(relu_s, TPG * H + t + 1)
                if t == 0 and not (isinstance(H, int) and H == 0):
                    dve.wait_ge(kv_mm, 2 * H)
                dve.tensor_scalar(q_ring[:, b % 2, g * TPG + t, :], Q[t % 2][:, 0:D], 0.0, None,
                                  ALU.max).then_inc(qpos_s, 1)
                dve.tensor_scalar(kf[:, t, :], Q[t % 2][:, D:QK], 0.0, None, ALU.max).then_inc(kpos_s, 1)

            def read_kv(b):
                dve.wait_ge(kv_mm, 2 * GPB * (b + 1))
                dve.wait_ge(prep_rows_in, 32 * b + 32)
                for h in range(DC):
                    dve.scalar_tensor_tensor(out=kvx[:, h, :], in0=bv_b[:, h * P:(h + 1) * P],
                                             scalar=KV[:, h * 256 + P:h * 256 + P + 1],
                                             in1=KV[:, h * 256:h * 256 + P],
                                             op0=ALU.mult, op1=ALU.add).then_inc(kv_rd, 1)
                    dve.tensor_scalar(ksr[:, h, :], ones[:, :], KV[:, h * 256 + P:h * 256 + P + 1], None,
                                      ALU.mult).then_inc(kv_rd, 1)
                dve.wait_ge(kv_rd, 4 * b + 4)
                for h in range(DC):
                    dve.tensor_tensor(kvm[:, h, :], kvx[:, h, :], mask[:, :], ALU.mult).then_inc(kv_ev, 1)

            def gate_m(b):
                dve.wait_ge(m_mm, b + 1)
                if not (isinstance(b, int) and b == 0):
                    dve.wait_ge(o_mm, 2 * GPB * b)
                dve.tensor_tensor(mg[:, :].rearrange("p (h n) -> p h n", h=DC),
                                  KV[:, :].rearrange("p (h n) -> p h n", h=DC),
                                  ga_b[:, :].unsqueeze(1).broadcast_to([P, DC, D]), ALU.mult).then_inc(mg_s, 1)

            def normaliser(J):
                dve.wait_ge(q_mul, TPG * J + TPG)
                dve.tensor_reduce(out=nrm[:, :], in_=qp[:, :, :].rearrange("p t (h e) -> p (t h) e", e=HD),
                                  axis=AX.X, op=ALU.add).then_inc(n_sum, 1)
                dve.wait_ge(n_sum, J + 1)
                dve.tensor_scalar(nre[:, :], nrm[:, :], ATT_EPS, None, ALU.add).then_inc(n_eps, 1)
                dve.wait_ge(n_eps, J + 1)
                dve.reciprocal(rno[:, :], nre[:, :]).then_inc(n_rec, 1)

            def add_x(J, pair, b, g, banks=(Q[0], V)):
                dve.wait_ge(o_mm, 2 * J + pair + 1)
                place = xr[:, b % XR, g * TPG + 2 * pair:g * TPG + 2 * pair + 2, :]
                dve.tensor_tensor(place, banks[pair][:, :].rearrange("p (t d) -> p t d", t=2), place,
                                  ALU.add).then_inc(x1_s, 1)

            def stats_b(J, pair, b, g):
                if pair == 0:
                    dve.tensor_copy(cur_b[:, g, :], cst[:, b, 2 * FC + DC:CW]).then_inc(curb_s, 1)
                stand_wait(dve, held, x1_s, 2 * J + pair + 1)
                for t in (2 * pair, 2 * pair + 1):
                    dve.bn_stats(st_b[:, t, :], xr[:, b % XR, g * TPG + t, :]).then_inc(stat_b, 1)
                stand_wait(dve, held, stat_b, TPG * J + 2 * pair + 2)
                for t in (2 * pair, 2 * pair + 1):
                    dve.bn_aggr(mv_b[:, t, :], st_b[:, t, :]).then_inc(aggr_b, 1)

            def apply_b(J, b, g):
                dve.wait_ge(rs_b_s, J + 1)
                if not (isinstance(J, int) and J == 0):
                    dve.wait_ge(tr_h, 2 * J)
                for t in range(TPG):
                    dve.tensor_scalar(xn_b[:, t, :], xr[:, b % XR, g * TPG + t, :], mv_b[:, t, 0:1],
                                      rs_b[:, t:t + 1], ALU.subtract, ALU.mult).then_inc(xn_b_s, 1)

            def h2_low(J, ch, g, banks=Q):
                dve.wait_ge(h2_hi_s, 2 * J + ch + 1)
                dve.scalar_tensor_tensor(out=h2_lo[:, g, ch, :], in0=banks[ch][:, :], scalar=cur_b[:, g, ch:ch + 1],
                                         in1=h2_hi[:, g, ch, :].bitcast(F32), op0=ALU.mult,
                                         op1=ALU.subtract).then_inc(h2_lo_s, 1)

            def whole_turns(c, f):
                dve.wait_ge(y_s, c + 1)
                if not (isinstance(c, int) and c < 2):
                    dve.wait_ge(fr_s, c - 1)
                dve.tensor_scalar(nt[:, f % 2, :], wk[:, f % 4, :], ROUND, ROUND, ALU.add,
                                  ALU.subtract).then_inc(kr_s, 1)

            def add_sine(c, f):
                dve.wait_ge(sn_s, c + 1)
                dve.scalar_tensor_tensor(out=wk[:, f % 4, :], in0=wk[:, f % 4, :], scalar=gcoef[:, f:f + 1],
                                         in1=U[f % 2][:, :], op0=ALU.mult, op1=ALU.add).then_inc(t_s, 1)

            def act_low(c, f):
                dve.wait_ge(ahi_s, c + 1)
                dve.scalar_tensor_tensor(out=a_lo[:, f % 2, :], in0=wk[:, f % 4, :], scalar=0.0,
                                         in1=a_hi[:, f % 2, :].bitcast(F32), op0=ALU.max,
                                         op1=ALU.subtract).then_inc(alo_s, 1)

            def gate_out(G, b):
                dve.wait_ge(f2_mm, FC * G + FC)
                dve.wait_ge(gb_in, 16 * b + 16)
                if not (isinstance(G, int) and G == 0):
                    dve.wait_ge(y_out, TPG * G)
                for p in range(2):
                    dve.tensor_tensor(zv[:, 2 * p:2 * p + 2, :], Y[p][:, :].rearrange("p (t d) -> p t d", t=2),
                                      gb_b[:, :].unsqueeze(1).broadcast_to([P, 2, D]),
                                      ALU.mult).then_inc(z_s, 1)

            def take_constants(b, g):
                dve.tensor_copy(cur_f[:, g, :], cst[:, b, 0:2 * FC]).then_inc(curf_s, 1)

            early_constants()
            stats_a(0, 0, 0)
            apply_a(0, 0, 0)
            stats_a(1, 0, 1)
            theta_in_turns()
            dve.wait_ge(wqkv_hi_s, 1)
            dve.tensor_tensor(wqkv_lo[:, :, :], stage_qkv, wqkv_hi[:, :, :].bitcast(F32), ALU.subtract) \
                .then_inc(wqkv_lo_s, 1)
            modulation()
            scale_a(0, 0)
            hT_low(0, 0, 0, U, h_early[0])
            hT_low(0, 1, 0, U, h_early[0])
            qkv_bias()
            apply_a(1, 0, 1)
            scale_a(0, 1)
            for H in range(AHEAD):
                b, g = H // GPB, H % GPB
                positive_part(H, 0, b, g)
                positive_part(H, 1, b, g)
                if H == 0:
                    gates()
                    rows_of_b2()
                if H == GPB:
                    read_kv(0)
                if H < AHEAD - 1:
                    hT_low(H + 1, 0, 1 - g, U, h_early[1 - g])
                    hT_low(H + 1, 1, 1 - g, U, h_early[1 - g])
                else:
                    add_x(0, 0, 0, 0, Y)
                    stats_b(0, 0, 0, 0)
                    add_x(0, 1, 0, 0, Y)
                    stats_b(0, 1, 0, 0)
                    normaliser(1)
                    apply_b(0, 0, 0)
                positive_part(H, 2, b, g)
                if H < AHEAD - 1:
                    positive_part(H, 3, b, g)
                if H == 0:
                    dve.wait_ge(w1_hi_s, 1)
                    dve.tensor_tensor(w1_lo[:, :, :], stage_w1, w1_hi[:, :, :].bitcast(F32), ALU.subtract) \
                        .then_inc(w1_lo_s, 1)
                if H < AHEAD - 2:
                    scale_a((H + 2) // GPB, g)
                    stats_a(H + 2, (H + 2) // GPB, g)
                    apply_a(H + 2, (H + 2) // GPB, g)
                if H == 1:
                    ffn_bias()
                if H == GPB:
                    gate_m(0)
                    dve.wait_ge(q_s, 2)
                    dve.wait_ge(prep_cp, 1)
                    times_ksum(dve, 0, 0)
                    normaliser(0)
                    dve.wait_ge(n_rec, 1)
                    over_norm(dve, 0, 0)
            take_constants(0, 0)
            h2_low(0, 0, 0, U)
            h2_low(0, 1, 0, U)
            dve.wait_ge(w2_hi_s, 1)
            dve.tensor_tensor(w2_lo[:, :, :], stage_w2, w2_hi[:, :, :].bitcast(F32), ALU.subtract) \
                .then_inc(w2_lo_s, 1)
            sine_factors()

            def window(b, g, do_a, do_b, do_kv):
                G = b * GPB + g
                J, H, C = G + 1, G + AHEAD, G * FC
                bj, gj = (b, 1) if g == 0 else (b + 1, 0)
                bh = b + LEAD
                before = (b, 0) if g else (b - 1, 1)
                first = is_first(b, g)
                late = int(not do_a)
                for f in range(FC):
                    c = C + f
                    if f == 0 and do_kv:
                        positive_part(H - 1, 3, b + LEAD - 1 if g == 0 else b + LEAD, 1 - g)
                    if f == 2 + late and do_b:
                        add_x(J, 0, bj, gj)
                    if f == 4 and do_a:
                        hT_low(H, 0, g)
                        hT_low(H, 1, g)
                    if f == 4 + late and do_b:
                        apply_b(J, bj, gj)
                    if f == 0 and g == 1 and not is_last(b):
                        gate_m(b + 1)
                    if not (first and f == 0):
                        add_sine(c - 1, (f - 1) % FC)
                    whole_turns(c, f)
                    if not (first and f < 2):
                        act_low(c - 2, (f - 2) % FC)
                    if f == 2 and not first:
                        gate_out(G - 1, before[0])
                    if f == 0 and do_a:
                        scale_a(bh, g)
                        stats_a(H, bh, g)
                    if f == 3 + late and do_b:
                        stats_b(J, 1, bj, gj)
                    if f == 1 and do_a:
                        apply_a(H, bh, g)
                    if f == 6 and do_a:
                        positive_part(H, 1, bh, g)
                    if f == 2 + late and do_b:
                        add_x(J, 1, bj, gj)
                    if f == 2 + late and do_b:
                        stats_b(J, 0, bj, gj)
                    if f == 5 and do_a:
                        positive_part(H, 0, bh, g)
                    if f == 7 and do_b and do_next(b, g):
                        normaliser(J + 1)
                    if f == 4 and g == 0 and not is_last(b):
                        read_kv(b + 1)
                    if f == 4 + late and do_b:
                        h2_low(J, 0, 1 - g)
                        h2_low(J, 1, 1 - g)
                    if f == 5 and not (is_last(b) and g == 1):
                        take_constants(bj, gj)
                    if f == 7 and do_a:
                        positive_part(H, 2, bh, g)

            windows(dve, window)
            add_sine(GROUPS * FC - 1, FC - 1)
            act_low(GROUPS * FC - 2, FC - 2)
            act_low(GROUPS * FC - 1, FC - 1)
            gate_out(GROUPS - 1, BATCH - 1)

        @block.tensor
        def _(pe):
            def passes(out, a, b, first, last):
                pe.matmul(out, a[0], b[0], start=first, stop=False)
                pe.matmul(out, a[0], b[1], start=False, stop=False)
                return pe.matmul(out, a[1], b[0], start=False, stop=last)

            def transpose_a(H, banks=Q):
                pe.wait_ge(xn_a_s, TPG * H + TPG)
                for ch in range(DC):
                    for t in range(TPG):
                        last = pe.transpose(banks[ch][:, t * P:(t + 1) * P], xn_a[:, t, ch * P:(ch + 1) * P],
                                            ident[:, :])
                    last.then_inc(tr_a, 1)

            def qk_bank_free(H, t):
                pe.wait_ge(kpos_s, TPG * H + t + 1)

            def project(H, t, b, h=hT):
                sl = slice(t * P, (t + 1) * P)
                for k in range(DC):
                    passes(Q[t % 2][:, :], (h[0][:, k, sl], h[1][:, k, sl]),
                           (wqkv_hi[:, k, 0:QK], wqkv_lo[:, k, 0:QK]), k == 0, False)
                if isinstance(b, int) and b == 0:
                    pe.wait_ge(rows_s, 2)
                    pe.matmul(Q[t % 2][:, :], ones2[0:1, :], sp_hi[0:1, 0:QK], start=False, stop=False)
                    last = pe.matmul(Q[t % 2][:, :], ones2[0:1, :], sp_lo[0:1, 0:QK], start=False, stop=True)
                else:
                    last = pe.matmul(Q[t % 2][:, :], ones2[:, :], qk_rows[:, b % 2, :], start=False, stop=True)
                last.then_inc(qk_mm, 1)
                for k in range(DC):
                    last = passes(V[:, (t % 2) * D:(t % 2 + 1) * D], (h[0][:, k, sl], h[1][:, k, sl]),
                                  (wqkv_hi[:, k, QK:QKV], wqkv_lo[:, k, QK:QKV]),
                                  t % 2 == 0 and k == 0, t % 2 == 1 and k == DC - 1)
                if t % 2:
                    last.then_inc(v_mm, 1)

            def sum_kv(H, pair, start, stop):
                pe.wait_ge(k_s, 2 * H + pair + 1)
                pe.wait_ge(v_s, 2 * H + pair + 1)
                for t in (2 * pair, 2 * pair + 1):
                    for h in range(DC):
                        last = pe.matmul(KV[:, h * 256:h * 256 + VW], kf[:, t, h * P:(h + 1) * P],
                                         v_sb[:, t, h, :], start=start and t == 0 and h == 0,
                                         stop=stop and t == TPG - 1 and h == DC - 1)
                last.then_inc(kv_mm, 1)

            def turn_kv(b):
                pe.wait_ge(kv_ev, 2 * b + 2)
                for h in range(DC):
                    pe.transpose(KV[:, h * P:(h + 1) * P], kvm[:, h, :], ident[:, :])
                for h in range(DC):
                    last = pe.matmul(KV[:, D + h * P:D + (h + 1) * P], ksr[:, h, :], ident[:, :],
                                     start=True, stop=True)
                last.then_inc(prep_tr, 1)

            def m_products(b):
                pe.wait_ge(prep_cp, b + 1)
                if isinstance(b, int) and b == 0:
                    pe.wait_ge(ld_wo, 16)
                for h in range(DC):
                    last = pe.matmul(KV[:, h * D:(h + 1) * D], kvT_ks[:, h * P:(h + 1) * P], wo_sb[:, h, :],
                                     start=True, stop=True)
                last.then_inc(m_mm, 1)

            def transpose_q(J, banks=Q):
                pe.wait_ge(q_sc, TPG * J + TPG)
                for ch in range(DC):
                    for t in range(TPG):
                        last = pe.transpose(banks[ch][:, t * P:(t + 1) * P], qp[:, t, ch * P:(ch + 1) * P],
                                            ident[:, :])
                    last.then_inc(tr_q, 1)

            def attention_out(J, pair, b, banks=(Q[0], V)):
                if pair == 0:
                    pe.wait_ge(qT_s, 2 * J + 2)
                    pe.wait_ge(mg_s, b + 1)
                    pe.wait_ge(o_rows_in, 16 * b + 16)
                o = banks[pair]
                pe.matmul(o[:, :], ones2[:, :], o_rows[:, :], start=True, stop=False)
                for t in range(2):
                    sl = slice((2 * pair + t) * P, (2 * pair + t + 1) * P)
                    for k in range(DC):
                        last = pe.matmul(o[:, t * D:(t + 1) * D], qT[:, k, sl], mg[:, k * D:(k + 1) * D],
                                         start=False, stop=t == 1 and k == DC - 1)
                last.then_inc(o_mm, 1)

            def transpose_h(J, banks=Q):
                pe.wait_ge(xn_b_s, TPG * J + TPG)
                for ch in range(DC):
                    for t in range(TPG):
                        last = pe.transpose(banks[ch][:, t * P:(t + 1) * P], xn_b[:, t, ch * P:(ch + 1) * P],
                                            ident[:, :])
                    last.then_inc(tr_h, 1)

            def ffn_up(c, G, g, f):
                if f == 0:
                    pe.wait_ge(h2_lo_s, 2 * G + 2)
                if not (isinstance(c, int) and c < 2):
                    pe.wait_ge(t_s, c - 1)
                fs = slice(f * P, (f + 1) * P)
                for k in range(DC):
                    last = passes(U[f % 2][:, :], (w1_hi[:, k, fs], w1_lo[:, k, fs]),
                                  (h2_hi[:, g, k, :], h2_lo[:, g, k, :]), k == 0, k == DC - 1)
                last.then_inc(f1_mm, 1)

            def ffn_down(c, G, f):
                pe.wait_ge(alo_s, c + 1)
                if isinstance(c, int) and c == 0:
                    pe.wait_ge(w2_lo_s, 1)
                    pe.wait_ge(b2_s, 2)
                if f == 0:
                    if not (isinstance(G, int) and G == 0):
                        pe.wait_ge(z_s, 2 * G)
                    for p in range(2):
                        pe.matmul(Y[p][:, :], ones2[:, :], b2_rows[:, :], start=True, stop=False)
                for t in range(TPG):
                    sl = slice(t * P, (t + 1) * P)
                    last = passes(Y[t // 2][:, (t % 2) * D:(t % 2 + 1) * D],
                                  (a_hi[:, f % 2, sl], a_lo[:, f % 2, sl]),
                                  (w2_hi[:, f, :], w2_lo[:, f, :]), False, f == FC - 1 and t % 2 == 1)
                last.then_inc(f2_mm, 1)

            pe.wait_ge(consts, 2)
            pe.wait_ge(ld_c, 16)
            for k in range(DC):
                last = pe.transpose(Y[0][:, k * BATCH:(k + 1) * BATCH], c8[:, k * P:(k + 1) * P],
                                    ident[0:BATCH, 0:BATCH])
            last.then_inc(turned, 1)
            pe.wait_ge(silu_s, 1)
            pe.wait_ge(ld_wm, 16)
            for j, off in enumerate((0, D, 3 * D, 4 * D)):
                for ch in range(DC):
                    at = (j * DC + ch) * BATCH
                    for k in range(DC):
                        last = pe.matmul(Q[1][:, at:at + BATCH], wm[:, k, off + ch * P:off + (ch + 1) * P],
                                         csil[:, k, :], start=(k == 0), stop=(k == DC - 1))
            last.then_inc(mod_mm, 1)
            pe.wait_ge(ld_th, 64)
            pe.transpose(Y[1][:, 0:4 * FC], th_rows, ident[0:4 * FC, 0:4 * FC]).then_inc(turned, 1)
            for i, off in enumerate((2 * D, 5 * D)):
                for k in range(DC):
                    last = pe.matmul(KV[0:BATCH, i * D:(i + 1) * D], csil[:, k, :], wm[:, k, off:off + D],
                                     start=(k == 0), stop=(k == DC - 1))
            last.then_inc(mod_mm, 1)
            transpose_a(0, U)
            pe.wait_ge(modT_s, 1)
            pe.wait_ge(ld_qkv, 48)
            for i, (o, off, n) in enumerate(((Y[0], 0, QK), (Y[1], QK, D))):
                for k in range(DC):
                    last = pe.matmul(o[0:BATCH, 0:n], modT[:, 0, k, :], stage_qkv[:, k, off:off + n],
                                     start=(k == 0), stop=(k == DC - 1))
                last.then_inc(bias_mm, 1)

            for H in range(AHEAD):
                b, g = H // GPB, H % GPB
                h = h_early[g]
                pe.wait_ge(hT_lo_s, 2 * H + 2)
                if b:
                    pe.wait_ge(qk_rows_in, 16 * b)
                if H == 0:
                    pe.wait_ge(wqkv_lo_s, 1)
                else:
                    qk_bank_free(H - 1, 2)
                    pe.wait_ge(v_s, 2 * H)
                project(H, 0, b, h)
                if H:
                    qk_bank_free(H - 1, 3)
                project(H, 1, b, h)
                if H == 3:
                    pe.wait_ge(mg_s, 1)
                if H:
                    sum_kv(H - 1, 0, H % 2 == 1, False)
                    sum_kv(H - 1, 1, False, H % 2 == 0)
                if H < AHEAD - 1:
                    transpose_a(H + 1, U)
                else:
                    transpose_q(0, U)
                if H == AHEAD - 1:
                    attention_out(0, 0, 0, Y)
                    attention_out(0, 1, 0, Y)
                qk_bank_free(H, 0)
                pe.wait_ge(v_s, 2 * H + 1)
                project(H, 2, b, h)
                if H == GPB:
                    turn_kv(0)
                qk_bank_free(H, 1)
                project(H, 3, b, h)
                if H == 0:
                    pe.wait_ge(ld_w1, 16)
                    for f in range(FC):
                        for k in range(DC):
                            last = pe.matmul(Y[0][:, f * BATCH:(f + 1) * BATCH], stage_w1[:, k, f * P:(f + 1) * P],
                                             modT[:, 2, k, :], start=(k == 0), stop=(k == DC - 1))
                    last.then_inc(b1_mm, 1)
                if H == GPB:
                    m_products(0)
            pe.wait_ge(qT_s, 2)
            transpose_h(0, U)

            def window(b, g, do_a, do_b, do_kv):
                G = b * GPB + g
                J, H, C = G + 1, G + AHEAD, G * FC
                bj = b if g == 0 else b + 1
                bh = b + LEAD
                first = is_first(b, g)
                late = int(not do_a)
                for f in range(FC):
                    c = C + f
                    ffn_up(c, G, g, f)
                    if f == 4 and do_kv:
                        sum_kv(H - 1, 1, False, g == 0)
                    if f == 2 + late and do_b:
                        if do_kv:
                            pe.wait_ge(v_s, 2 * H)
                        attention_out(J, 1, bj)
                    if f == 6 and do_a:
                        project(H, 1, bh)
                    if f == 7 and g == 0 and not is_last(b):
                        m_products(b + 1)
                    if not (first and f < 3):
                        ffn_down(c - 3, G - (f < 3), (f - 3) % FC)
                    if f == late and do_b:
                        if do_kv:
                            qk_bank_free(H - 1, TPG - 1)
                        transpose_q(J)
                    if f == 1 + late and do_b:
                        attention_out(J, 0, bj)
                    if f == 5 and g == 0 and not is_last(b):
                        turn_kv(b + 1)
                    if f == 6 and do_a:
                        qk_bank_free(H, 0)
                        pe.wait_ge(v_s, 2 * H + 1)
                        project(H, 2, bh)
                    if f == 3 and do_a:
                        pe.wait_ge(x1_s, 2 * J + 1)
                        transpose_a(H)
                    if f == 2 and do_kv:
                        if g == 1:
                            pe.wait_ge(mg_s, b + 2)
                        sum_kv(H - 1, 0, g == 1, False)
                    if f == 5 and do_a:
                        pe.wait_ge(qk_rows_in, 16 * (b + LEAD))
                        pe.wait_ge(h2_lo_s, 2 * J + 2)
                        pe.wait_ge(x1_s, 2 * J + 2)
                        project(H, 0, bh)
                    if f == 4 + late and do_b:
                        if do_a:
                            pe.wait_ge(hT_lo_s, 2 * H + 2)
                        transpose_h(J)
                    if f == 7 and do_a:
                        qk_bank_free(H, 1)
                        project(H, 3, bh)

            pe.wait_ge(w1_lo_s, 1)

            windows(pe, window)
            for f in range(FC - 3, FC):
                ffn_down((GROUPS - 1) * FC + f, GROUPS - 1, f)


_INS = ["L0_attn_x", "L0_attn_Wq", "L0_attn_bq", "L0_attn_Wk", "L0_attn_bk", "L0_attn_Wv", "L0_attn_bv",
        "L0_attn_Wo", "L0_attn_bo", "L0_ffn_W1", "L0_ffn_b1", "L0_ffn_quantum_phases",
        "L0_ffn_quantum_weights_real", "L0_ffn_quantum_weights_imag", "L0_ffn_W2", "L0_ffn_b2",
        "L0_c", "L0_wmod"]


def kernel(**inputs):
    import numpy as _np
    import concourse.bacc as _bacc
    from concourse import mybir as _mybir
    from concourse.bass_utils import run_bass_kernel_spmd as _run

    nc = _bacc.Bacc("TRN2", target_bir_lowering=False, num_devices=1)
    arrays, args = {}, []
    for name in _INS:
        a = _np.ascontiguousarray(inputs[name])
        arrays[f"in_{name}"] = a
        args.append(nc.dram_tensor(f"in_{name}", a.shape, _mybir.dt.from_np(a.dtype), kind="ExternalInput").ap())
    args.append(nc.dram_tensor("out", (BATCH, SEQ, D), _mybir.dt.float32, kind="ExternalOutput").ap())
    adaln_block(nc, *args)
    r = _run(nc, [arrays], core_ids=[0])
    return r.results[0]["out"]
```
